# Optimizing a Trainium2 kernel written in Bass

```python
import numpy as np
import jax
import jax.numpy as jnp

def _softmax(x, axis=-1):
    return jax.nn.softmax(x, axis=axis)

def _gelu(x):
    return jax.nn.gelu(x, approximate=True)

def _silu(x):
    return jax.nn.silu(x)

def _sigmoid(x):
    return jax.nn.sigmoid(x)

def _layernorm(x, axis=-1, eps=1e-05):
    m = jnp.mean(x, axis=axis, keepdims=True)
    v = jnp.var(x, axis=axis, keepdims=True)
    return (x - m) / jnp.sqrt(v + eps)

def _scatter_add(tgt, idx, src, axis=0):
    return tgt.at[idx].add(src)

def _segment_sum(src, seg, n):
    return jax.ops.segment_sum(src, seg, n)
kernel_name = 'mk_adaln_d1_jaxref_r8_544310'

def setup_inputs(seed: int=0):
    np.random.seed(seed)
    _w = jnp.asarray

    def _L0_attn_setup():
        import jax, jax.numpy as jnp
        import numpy as np
        LN_EPS = 1e-05

        def _layernorm(x, g, b):
            mu = jnp.mean(x, axis=-1, keepdims=True)
            var = jnp.var(x, axis=-1, keepdims=True)
            return (x - mu) * jax.lax.rsqrt(var + LN_EPS) * g + b
        key = jax.random.key(seed)
        B, S, D, H = (2, 256, 128, 16)
        dh = D // H
        r = 48
        r_out = 96
        I = 4 * D
        r_mlp = 64
        ks = jax.random.split(key, 24)
        sc = lambda *sh: 0.02
        inp = {'hidden_states': jax.random.normal(ks[0], (B, S, D), jnp.float32), 'ln1_g': jnp.ones((D,), jnp.float32), 'ln1_b': jnp.zeros((D,), jnp.float32), 'ln2_g': jnp.ones((D,), jnp.float32), 'ln2_b': jnp.zeros((D,), jnp.float32), 'q_U': jax.random.normal(ks[1], (D, H, r), jnp.float32) * 0.02, 'q_V': jax.random.normal(ks[2], (H, r, dh), jnp.float32) * 0.02, 'q_b': jax.random.normal(ks[3], (H, dh), jnp.float32) * 0.02, 'k_U': jax.random.normal(ks[4], (D, H, r), jnp.float32) * 0.02, 'k_V': jax.random.normal(ks[5], (H, r, dh), jnp.float32) * 0.02, 'k_b': jax.random.normal(ks[6], (H, dh), jnp.float32) * 0.02, 'v_U': jax.random.normal(ks[7], (D, H, r), jnp.float32) * 0.02, 'v_V': jax.random.normal(ks[8], (H, r, dh), jnp.float32) * 0.02, 'v_b': jax.random.normal(ks[9], (H, dh), jnp.float32) * 0.02, 'out_U': jax.random.normal(ks[10], (D, r_out), jnp.float32) * 0.02, 'out_V': jax.random.normal(ks[11], (r_out, D), jnp.float32) * 0.02, 'out_b': jnp.zeros((D,), jnp.float32), 'fc1_U': jax.random.normal(ks[12], (D, r_mlp), jnp.float32) * 0.02, 'fc1_V': jax.random.normal(ks[13], (r_mlp, I), jnp.float32) * 0.02, 'fc1_b': jnp.zeros((I,), jnp.float32), 'fc2_U': jax.random.normal(ks[14], (I, r_mlp), jnp.float32) * 0.02, 'fc2_V': jax.random.normal(ks[15], (r_mlp, D), jnp.float32) * 0.02, 'fc2_b': jnp.zeros((D,), jnp.float32)}
        return inp
    _L0_attn_in = _L0_attn_setup()

    def _L0_ffn_setup():
        import jax, jax.numpy as jnp
        import numpy as np
        D, H, O, E, TOPK = (128, 512, 128, 8, 2)
        B, S = (4, 128)
        key = jax.random.key(seed)
        ks = jax.random.split(key, 12)
        std = 0.02
        return {'hidden_states': jax.random.normal(ks[0], (B, S, D), dtype=jnp.float32), 'norm_weight': jnp.ones((D,), dtype=jnp.float32), 'router_w': jax.random.normal(ks[1], (E, D), dtype=jnp.float32) * std, 'sw1': jax.random.normal(ks[2], (D, H), dtype=jnp.float32) * (1.0 / np.sqrt(D)), 'sb1': jnp.zeros((H,), dtype=jnp.float32), 'sw2': jax.random.normal(ks[3], (H, O), dtype=jnp.float32) * (1.0 / np.sqrt(H)), 'sb2': jnp.zeros((O,), dtype=jnp.float32), 'ew1': jax.random.normal(ks[4], (E, D, H), dtype=jnp.float32) * (1.0 / np.sqrt(D)), 'eb1': jnp.zeros((E, H), dtype=jnp.float32), 'ew2': jax.random.normal(ks[5], (E, H, O), dtype=jnp.float32) * (1.0 / np.sqrt(H)), 'eb2': jnp.zeros((E, O), dtype=jnp.float32)}
    _L0_ffn_in = _L0_ffn_setup()
    _L0_c = _w((lambda *s: np.random.randn(*s).astype(np.float32) * 0.05)(8, 128))
    _L0_wmod = _w((lambda *s: np.random.randn(*s).astype(np.float32) * 0.05)(128, 6 * 128) * 128 ** (-0.5))
    _d = {'L0_attn_hidden_states': _L0_attn_in['hidden_states'], 'L0_attn_ln1_g': _L0_attn_in['ln1_g'], 'L0_attn_ln1_b': _L0_attn_in['ln1_b'], 'L0_attn_ln2_g': _L0_attn_in['ln2_g'], 'L0_attn_ln2_b': _L0_attn_in['ln2_b'], 'L0_attn_q_U': _L0_attn_in['q_U'], 'L0_attn_q_V': _L0_attn_in['q_V'], 'L0_attn_q_b': _L0_attn_in['q_b'], 'L0_attn_k_U': _L0_attn_in['k_U'], 'L0_attn_k_V': _L0_attn_in['k_V'], 'L0_attn_k_b': _L0_attn_in['k_b'], 'L0_attn_v_U': _L0_attn_in['v_U'], 'L0_attn_v_V': _L0_attn_in['v_V'], 'L0_attn_v_b': _L0_attn_in['v_b'], 'L0_attn_out_U': _L0_attn_in['out_U'], 'L0_attn_out_V': _L0_attn_in['out_V'], 'L0_attn_out_b': _L0_attn_in['out_b'], 'L0_attn_fc1_U': _L0_attn_in['fc1_U'], 'L0_attn_fc1_V': _L0_attn_in['fc1_V'], 'L0_attn_fc1_b': _L0_attn_in['fc1_b'], 'L0_attn_fc2_U': _L0_attn_in['fc2_U'], 'L0_attn_fc2_V': _L0_attn_in['fc2_V'], 'L0_attn_fc2_b': _L0_attn_in['fc2_b'], 'L0_ffn_norm_weight': _L0_ffn_in['norm_weight'], 'L0_ffn_router_w': _L0_ffn_in['router_w'], 'L0_ffn_sw1': _L0_ffn_in['sw1'], 'L0_ffn_sb1': _L0_ffn_in['sb1'], 'L0_ffn_sw2': _L0_ffn_in['sw2'], 'L0_ffn_sb2': _L0_ffn_in['sb2'], 'L0_ffn_ew1': _L0_ffn_in['ew1'], 'L0_ffn_eb1': _L0_ffn_in['eb1'], 'L0_ffn_ew2': _L0_ffn_in['ew2'], 'L0_ffn_eb2': _L0_ffn_in['eb2'], 'L0_c': _L0_c, 'L0_wmod': _L0_wmod}
    _x0 = _d['L0_attn_hidden_states']
    _d['L0_attn_hidden_states'] = jax.random.normal(jax.random.fold_in(jax.random.key(seed), 1), (8, 512, 128), dtype=_x0.dtype)
    del _x0
    return _d

def reference(L0_attn_hidden_states, L0_attn_ln1_g, L0_attn_ln1_b, L0_attn_ln2_g, L0_attn_ln2_b, L0_attn_q_U, L0_attn_q_V, L0_attn_q_b, L0_attn_k_U, L0_attn_k_V, L0_attn_k_b, L0_attn_v_U, L0_attn_v_V, L0_attn_v_b, L0_attn_out_U, L0_attn_out_V, L0_attn_out_b, L0_attn_fc1_U, L0_attn_fc1_V, L0_attn_fc1_b, L0_attn_fc2_U, L0_attn_fc2_V, L0_attn_fc2_b, L0_ffn_norm_weight, L0_ffn_router_w, L0_ffn_sw1, L0_ffn_sb1, L0_ffn_sw2, L0_ffn_sb2, L0_ffn_ew1, L0_ffn_eb1, L0_ffn_ew2, L0_ffn_eb2, L0_c, L0_wmod):

    def _L0_attn_ref(hidden_states, ln1_g, ln1_b, ln2_g, ln2_b, q_U, q_V, q_b, k_U, k_V, k_b, v_U, v_V, v_b, out_U, out_V, out_b, fc1_U, fc1_V, fc1_b, fc2_U, fc2_V, fc2_b):
        import jax, jax.numpy as jnp
        import numpy as np
        LN_EPS = 1e-05

        def _layernorm(x, g, b):
            mu = jnp.mean(x, axis=-1, keepdims=True)
            var = jnp.var(x, axis=-1, keepdims=True)
            return (x - mu) * jax.lax.rsqrt(var + LN_EPS) * g + b
        B, S, D = hidden_states.shape
        H, dh = (q_V.shape[0], q_V.shape[2])
        x = _layernorm(hidden_states, ln1_g, ln1_b)
        Q = jnp.einsum('bsd,dhr,hre->bhse', x, q_U, q_V) + q_b[None, :, None, :]
        Pk = jnp.einsum('bsd,dhr->bhsr', x, k_U)
        Pv = jnp.einsum('bsd,dhr->bhsr', x, v_U)
        K = jnp.einsum('bhsr,hrd->bhsd', Pk, k_V) + k_b[None, :, None, :]
        V = jnp.einsum('bhsr,hrd->bhsd', Pv, v_V) + v_b[None, :, None, :]
        scale = 1.0 / jnp.sqrt(jnp.asarray(dh, x.dtype))
        scores = jnp.einsum('bhse,bhte->bhst', Q, K) * scale
        causal = jnp.tril(jnp.ones((S, S), bool))
        scores = jnp.where(causal[None, None], scores, jnp.asarray(-1000000000.0, scores.dtype))
        attn = jax.nn.softmax(scores, axis=-1)
        ctx = jnp.einsum('bhst,bhtd->bhsd', attn, V)
        ctx = ctx.transpose(0, 2, 1, 3).reshape(B, S, D)
        attn_out = ctx @ out_U @ out_V + out_b
        h = hidden_states + attn_out
        x2 = _layernorm(h, ln2_g, ln2_b)
        hmid = jax.nn.gelu(x2 @ fc1_U @ fc1_V + fc1_b, approximate=True)
        mlp_out = hmid @ fc2_U @ fc2_V + fc2_b
        return h + mlp_out

    def _L0_ffn_ref(hidden_states, norm_weight, router_w, sw1, sb1, sw2, sb2, ew1, eb1, ew2, eb2):
        import jax, jax.numpy as jnp
        import numpy as np
        D, H, O, E, TOPK = (128, 512, 128, 8, 2)
        B, S = (4, 128)
        b, s, d = hidden_states.shape
        var = jnp.mean(jnp.square(hidden_states), axis=-1, keepdims=True)
        normed = hidden_states * jax.lax.rsqrt(var + 1e-08) * norm_weight
        shared = jnp.maximum(normed @ sw1 + sb1, 0.0) @ sw2 + sb2
        flat = normed.reshape(-1, d)
        T = flat.shape[0]
        probs = jax.nn.sigmoid(flat @ router_w.T)
        scores, idx = jax.lax.top_k(probs, TOPK)
        w = scores / (jnp.sum(scores, axis=-1, keepdims=True) + 1e-06)
        comb = jnp.zeros((T, E), dtype=flat.dtype)
        comb = comb.at[jnp.arange(T)[:, None], idx].add(w)
        h = jnp.maximum(jnp.einsum('td,edh->teh', flat, ew1) + eb1[None, :, :], 0.0)
        eo = jnp.einsum('teh,eho->teo', h, ew2) + eb2[None, :, :]
        routed = jnp.einsum('teo,te->to', eo, comb)
        return shared + routed.reshape(b, s, -1)
    x = L0_attn_hidden_states
    mod = (_silu(L0_c) @ L0_wmod).reshape(L0_c.shape[0], 6, 1, -1)
    sa, ca, ga, sb, cb, gb = (mod[:, 0], mod[:, 1], mod[:, 2], mod[:, 3], mod[:, 4], mod[:, 5])
    ga = (2 * (ga >= 0) - 1) * jnp.maximum(jnp.abs(ga), 0.25)
    gb = (2 * (gb >= 0) - 1) * jnp.maximum(jnp.abs(gb), 0.25)
    h = _layernorm(x, axis=-1) * (1 + ca) + sa
    x = x + ga * _L0_attn_ref(h, L0_attn_ln1_g, L0_attn_ln1_b, L0_attn_ln2_g, L0_attn_ln2_b, L0_attn_q_U, L0_attn_q_V, L0_attn_q_b, L0_attn_k_U, L0_attn_k_V, L0_attn_k_b, L0_attn_v_U, L0_attn_v_V, L0_attn_v_b, L0_attn_out_U, L0_attn_out_V, L0_attn_out_b, L0_attn_fc1_U, L0_attn_fc1_V, L0_attn_fc1_b, L0_attn_fc2_U, L0_attn_fc2_V, L0_attn_fc2_b)
    h = _layernorm(x, axis=-1) * (1 + cb) + sb
    x = x + gb * _L0_ffn_ref(h, L0_ffn_norm_weight, L0_ffn_router_w, L0_ffn_sw1, L0_ffn_sb1, L0_ffn_sw2, L0_ffn_sb2, L0_ffn_ew1, L0_ffn_eb1, L0_ffn_ew2, L0_ffn_eb2)
    return x

_drawn_inputs = setup_inputs


def setup_inputs(seed=0):
    import zlib

    import numpy as np

    out = dict(_drawn_inputs(seed))
    spreads = {'L0_attn_ln1_g': (1.0, 0.6),
     'L0_attn_ln1_b': (0.0, 0.8),
     'L0_attn_ln2_g': (1.0, 0.6),
     'L0_attn_ln2_b': (0.0, 0.8),
     'L0_attn_out_b': (0.0, 0.684),
     'L0_attn_fc1_b': (0.0, 0.8),
     'L0_attn_fc2_b': (0.0, 0.8),
     'L0_ffn_norm_weight': (1.0, 0.6),
     'L0_ffn_sb1': (0.0, 1.781),
     'L0_ffn_sb2': (0.0, 1.126),
     'L0_ffn_eb1': (0.0, 2.0),
     'L0_ffn_eb2': (0.0, 1.785)}
    factors = {'L0_attn_q_U': 8.0,
     'L0_attn_q_V': 8.0,
     'L0_attn_q_b': 8.0,
     'L0_attn_k_U': 8.0,
     'L0_attn_k_V': 8.0,
     'L0_attn_k_b': 64.0,
     'L0_attn_v_U': 8.0,
     'L0_attn_v_V': 8.0,
     'L0_attn_v_b': 8.0,
     'L0_attn_out_U': 8.0,
     'L0_attn_out_V': 8.0,
     'L0_attn_fc1_U': 8.0,
     'L0_attn_fc1_V': 8.0,
     'L0_attn_fc2_U': 8.0,
     'L0_attn_fc2_V': 8.0}
    for name, (base, spread) in spreads.items():
        noise = np.random.default_rng([zlib.crc32(name.encode()), seed]).standard_normal(out[name].shape)
        drawn = base * np.exp(spread * noise) if base else spread * noise
        out[name] = jnp.asarray(drawn.astype(out[name].dtype))
    for name, factor in factors.items():
        out[name] = (out[name] * factor).astype(out[name].dtype)
    return out
```

```python
from contextlib import ExitStack

import concourse.bass as bass
from concourse import mybir

F32 = mybir.dt.float32
BF16 = mybir.dt.bfloat16
U32 = mybir.dt.uint32
I32 = mybir.dt.int32
ALU = mybir.AluOpType
ACT = mybir.ActivationFunctionType
AXIS = mybir.AxisListType

P = 128
B, S, D = 8, 512, 128
NT = S // P
HEADS, DH = 16, 8
RANK, PAIRS = 48, HEADS // 2
R_OUT, R_MLP = 96, 64
FF = 4 * D
NF = FF // P
E = 8
GROUPS, JH = 4, 4
PRODUCTS = [(0, 0), (0, 1), (0, 2), (1, 0), (1, 1), (2, 0)]
SROWS = DH * len(PRODUCTS)
MROWS = 3
SCALE = float(DH) ** -0.5
LN_EPS, RMS_EPS = 1e-5, 1e-8
MASKED = -1e30

SLOTS = 256
N_TILES = B * S * 2 // SLOTS + E
N_SLOTS = N_TILES * SLOTS
ROW = D + 4

S1_UNITS = [(0, [0, 1, 2, 3]), (1, [0, 1]), (1, [2, 3])] + [(i, [j]) for i in (2, 3) for j in range(JH)]
S2_UNITS = [(0, [0, 1]), (0, [2, 3]), (1, [0, 1]), (1, [2, 3]), (2, [0, 1, 2, 3]), (3, [0, 1, 2, 3])]
NS1, NS2 = len(S1_UNITS), len(S2_UNITS)
KT_LEN = [S - P * k for k in range(NT)]
KT_OFF = [JH * sum(KT_LEN[:k]) for k in range(NT)]
PT_LEN = JH * sum(KT_LEN)

BANK_USES = ["T", "M3", "Q", "K", "M0", "V", "M1", "M2", "O"]
FIRST_STEP = -3


class Step:

    def __init__(self, t, phase, count=B):
        self.t, self.phase, self.count, self.steady = t, phase, count, not isinstance(t, int)

    def has(self, lag):
        return self.steady or 0 <= self.t + lag < self.count

    def buffer(self, lag, n=2):
        return (self.phase + lag) % n

    def uses(self, use):
        return self.has({"T": 2, "Q": 2, "K": 2, "V": 2, "M3": 0, "O": -1}.get(use, 1))

    def number(self, use):
        if self.steady:
            return (self.t - 1) * len(BANK_USES) + Step(1, 0).number(use)
        before = sum(Step(u, 0).uses(k) for u in range(FIRST_STEP, self.t) for k in BANK_USES)
        return before + sum(self.uses(k) for k in BANK_USES[:BANK_USES.index(use)])


def wait(eng, sem, value):
    if not isinstance(value, int) or value > 0:
        eng.wait_ge(sem, value)


def worked_out(eng, value):
    if not isinstance(value, int):
        eng.compute_val(value)
    return value


def wait_apart(eng, sem, value, done):
    value = worked_out(eng, value)
    eng.wait_ge(done, 1)
    wait(eng, sem, value)


def pipeline(eng, body, first, last, loop_from, loop_to, unroll=2, count=B):
    for t in range(first, loop_from):
        body(Step(t, t % unroll, count))
    with eng.Fori(loop_from, loop_to - unroll + 1, unroll) as t:
        for k in range(unroll):
            body(Step(t + k, (loop_from + k) % unroll, count))
    for t in range(loop_to, last + 1):
        body(Step(t, t % unroll, count))


def steps(eng, body):
    pipeline(eng, body, FIRST_STEP, B, 1, 5)

COLS = {}
N_COLS = 0
for _name, _n in (("ln1_g", 1), ("ln1_b", 1), ("q_b", 1), ("k_b", 1), ("v_b", 1), ("ln2_g", 1), ("ln2_b", 1),
                  ("norm_w", 1), ("fc1_b", NF), ("sb1", NF), ("eb1", E * NF)):
    COLS[_name] = N_COLS
    N_COLS += _n


def adaln_block(nc, a, out):
    ctx = ExitStack()
    with ctx:
        def sb(name, shape, dt=F32, until=ctx):
            return until.enter_context(nc.sbuf_tensor(name, shape, dt))

        def pb(name, shape):
            return ctx.enter_context(nc.psum_tensor(name, shape, F32))

        def sem(name):
            return ctx.enter_context(nc.semaphore(name))

        def dram(name, shape, dt=F32):
            return nc.dram_tensor(name, shape, dt, kind="Internal").ap()

        x_sb = sb("x_sb", [P, B * NT, D])
        h_sb = sb("h_sb", [P, B * NT, D])
        w_qkv = sb("w_qkv", [P, 3, D])
        w_out = sb("w_out", [P, D])
        w_fc1 = sb("w_fc1", [P, FF])
        w_fc2 = sb("w_fc2", [P, NF, D])
        cols = sb("cols", [P, N_COLS])
        out_bias = sb("out_bias", [P, D])
        ident = sb("ident", [P, P])
        ident_b = sb("ident_b", [P, P], BF16)
        later_q = sb("later_q", [P, JH, P], BF16)
        later_k = sb("later_k", [P, JH, P], BF16)
        head_rows = sb("head_rows", [HEADS, P])
        zeros = sb("zeros", [P, P])
        half_neg = sb("half_neg", [P, NT])
        ln_eps = sb("ln_eps", [P, NT])
        rms_eps = sb("rms_eps", [P, NT])
        v_zeroed = sem("v_zeroed")
        n3x = sb("n3x", [P, B * NT, ROW])
        slots = sb("slots", [P, 2, B * NT], U32)
        picked_w = sb("picked_w", [P, 2, B * NT])
        tile_expert = sb("tile_expert", [P, N_TILES], U32)

        front = ctx.enter_context(ExitStack())
        work = sb("work", [P, 2 * PT_LEN], until=front)

        q_st = sb("q_st", [P, HEADS, S], BF16, until=front)
        k_st = sb("k_st", [P, HEADS, S], BF16, until=front)
        v_sb = sb("v_sb", [P, NT, HEADS, 32], until=front)
        mod_sb = sb("mod_sb", [P, B, 2 * D], until=front)

        ps_s2 = pb("ps_s2", [P, 4, 512])
        ps_s1 = pb("ps_s1", [P, 2, 512])
        ps_pv = pb("ps_pv", [P, 512])
        ps_m = pb("ps_m", [P, 512])

        mod_d = dram("mod_d", (B, 6 * D))
        q_d = dram("q_d", (2, len(PRODUCTS), P, S), BF16)
        k_d = dram("k_d", (2, len(PRODUCTS), P, S), BF16)
        max_d = dram("max_d", (GROUPS, MROWS, JH, NT, P), BF16)
        sum_d = dram("sum_d", (HEADS, S))
        rec_d = dram("rec_d", (HEADS, S))

        out_tok = out.rearrange("b (i p) d -> p (b i) d", p=P)
        x_tok = a["x"].rearrange("b (i p) d -> p (b i) d", p=P)

        def col(name, k=0):
            return cols[:, COLS[name] + k:COLS[name] + k + 1]

        def setup():
            n_u = 3 * PAIRS * D
            u_t = work[0:2 * RANK, 0:n_u].rearrange("p (m k d) -> p m k d", m=3, k=PAIRS)
            at = n_u
            v_bd = work[0:2 * RANK, at:at + 3 * PAIRS * 16].rearrange("p (m k c) -> p m k c", m=3, k=PAIRS)
            at += 3 * PAIRS * 16
            out_ut = work[0:R_OUT, at:at + D]
            out_v = work[0:R_OUT, at + D:at + 2 * D]
            at += 2 * D
            fc1_ut = work[0:R_MLP, at:at + D]
            fc2_v = work[0:R_MLP, at + D:at + 2 * D]
            at += 2 * D
            fc1_v = work[0:R_MLP, at:at + FF]
            fc2_ut = work[0:R_MLP, at + FF:at + 2 * FF]
            at += 2 * FF
            w_mod = work[:, at:at + 6 * D]
            at += 6 * D
            mod = work[0:B, at:at + 6 * D].rearrange("b (k d) -> b k d", d=D)
            at += 6 * D
            vb_wide = work[:, at:at + D]
            out_b_all = work[:, at + D:at + 2 * D]
            at += 2 * D
            gate_sign = work[0:B, at:at + 2 * D].rearrange("b (k d) -> b k d", d=D)
            gate_abs = work[0:B, at + 2 * D:at + 4 * D].rearrange("b (k d) -> b k d", d=D)
            at += 4 * D
            c_t, c_exp, c_one, c_rec, c_silu = (work[:, at + B * k:at + B * (k + 1)] for k in range(5))

            c_loaded, w_loaded, x_loaded = sem("c_loaded"), sem("w_loaded"), sem("x_loaded")
            c_exped, c_steps, silu_ready = sem("c_exped"), sem("c_steps"), sem("silu_ready")
            mod_done, mod_copied, mod_steps, mod_ready = sem("mod_done"), sem("mod_copied"), sem("mod_steps"), sem("mod_ready")
            mod_stored, mod_spread, pairs_done, small_done = sem("mod_stored"), sem("mod_spread"), sem("pairs_done"), sem("small_done")
            w_out_ready, bias_done, consts, consts2 = sem("w_out_ready"), sem("bias_done"), sem("consts"), sem("consts2")
            all_copied = sem("all_copied")
            n_weight_loads = 2 + 6 + 1 + 6
            with nc.Block() as block:
                @block.sync
                def _(sp):
                    sp.dma_start(c_t, a["c_t"]).then_inc(c_loaded, 16)
                    sp.dma_start(w_mod, a["w_mod"]).then_inc(c_loaded, 16)
                    sp.dma_start(cols[:], a["cols"]).then_inc(w_loaded, 16)
                    sp.dma_start(u_t, a["u_t"]).then_inc(w_loaded, 16)
                    sp.wait_ge(v_zeroed, 1)
                    for hh in range(2):
                        for m in range(3):
                            sp.dma_start(v_bd[hh * RANK:(hh + 1) * RANK, m, :, hh * DH:(hh + 1) * DH],
                                         a["v_pairs"][hh, :, m]).then_inc(w_loaded, 16)
                    sp.dma_start(out_b_all, a["out_b"].partition_broadcast(P)).then_inc(w_loaded, 16)
                    for dst, name in ((out_ut, "out_ut"), (out_v, "out_v"), (fc1_ut, "fc1_ut"), (fc1_v, "fc1_v"),
                                      (fc2_ut, "fc2_ut"), (fc2_v, "fc2_v")):
                        sp.dma_start(dst, a[name]).then_inc(w_loaded, 16)
                    for b in range(B):
                        sp.dma_start(x_sb[:, NT * b:NT * (b + 1), :], x_tok[:, NT * b:NT * (b + 1), :])\
                            .then_inc(x_loaded, 16)
                    sp.wait_ge(mod_ready, 4)
                    sp.dma_start(mod_d, mod.rearrange("b k d -> b (k d)")).then_inc(mod_stored, 16)
                    sp.wait_ge(mod_stored, 16)
                    sp.dma_start(mod_sb[:], mod_d[:, 0:2 * D].partition_broadcast(P)).then_inc(mod_spread, 16)
                    sp.wait_ge(mod_spread, 16)
                    sp.wait_ge(x_loaded, 16 * B)

                @block.gpsimd
                def _(pool):
                    pool.memset(ident[:], 0.0).then_inc(consts, 1)
                    pool.memset(later_q[:], 0.0).then_inc(consts, 1)
                    pool.memset(later_k[:], 0.0).then_inc(consts, 1)
                    pool.memset(head_rows[:], 1.0).then_inc(consts, 1)
                    pool.memset(half_neg[:], -0.5).then_inc(consts, 1)
                    pool.memset(ln_eps[:], LN_EPS).then_inc(consts, 1)
                    pool.memset(rms_eps[:], RMS_EPS).then_inc(consts, 1)
                    pool.wait_ge(consts, 7)
                    pool.affine_select(out=ident[:], in_=ident[:], compare_op=ALU.not_equal, fill=1.0, base=0,
                                       pattern=[[-1, P]], channel_multiplier=1).then_inc(consts2, 1)
                    pool.affine_select(out=later_q[:], in_=later_q[:], compare_op=ALU.is_ge, fill=MASKED, base=0,
                                       pattern=[[0, JH], [-1, P]], channel_multiplier=1).then_inc(consts2, 1)
                    pool.affine_select(out=later_k[:], in_=later_k[:], compare_op=ALU.is_ge, fill=MASKED, base=0,
                                       pattern=[[0, JH], [1, P]], channel_multiplier=-1).then_inc(consts2, 1)
                    pool.affine_select(out=head_rows[:], in_=head_rows[:], compare_op=ALU.is_ge, fill=0.0, base=0,
                                       pattern=[[1, P]], channel_multiplier=-DH).then_inc(consts2, 1)
                    pool.wait_ge(consts2, 4)
                    pool.affine_select(out=head_rows[:], in_=head_rows[:], compare_op=ALU.is_ge, fill=0.0,
                                       base=DH - 1, pattern=[[-1, P]], channel_multiplier=DH).then_inc(consts2, 1)
                    pool.tensor_copy(ident_b[:], ident[:]).then_inc(consts2, 1)
                    pool.memset(v_sb[:], 1.0).then_inc(consts2, 1)

                @block.scalar
                def _(act):
                    act.wait_ge(c_loaded, 32)
                    act.activation(c_exp, c_t, ACT.Exp, scale=-1.0).then_inc(c_exped, 1)

                @block.tensor
                def _(pe):
                    pe.wait_ge(silu_ready, 1)
                    pe.matmul(ps_m[0:B, :], c_silu, w_mod[:, 0:512], start=True, stop=True)
                    pe.matmul(ps_pv[0:B, 0:256], c_silu, w_mod[:, 512:768], start=True, stop=True).then_inc(mod_done, 1)
                    pe.wait_ge(w_loaded, 16 * n_weight_loads)
                    for m in range(3):
                        for k in range(PAIRS):
                            mm = pe.matmul(ps_s2[:, m, 16 * k:16 * k + 16], u_t[:, m, k, :], v_bd[:, m, k, :],
                                           start=True, stop=True)
                    mm.then_inc(pairs_done, 1)
                    pe.matmul(ps_s1[:, 0, 0:D], out_ut, out_v, start=True, stop=True)
                    pe.matmul(ps_s1[:, 1, :], fc1_ut, fc1_v, start=True, stop=True)
                    for k in range(NF):
                        mm = pe.matmul(ps_s2[:, 3, k * P:(k + 1) * P], fc2_ut[:, k * P:(k + 1) * P], fc2_v,
                                       start=True, stop=True)
                    mm.then_inc(small_done, 1)
                    pe.wait_ge(w_out_ready, 2)
                    pe.wait_ge(mod_copied, 2)
                    pe.matmul(ps_m[:, 0:D], vb_wide, w_out[:], start=True, stop=True).then_inc(bias_done, 1)

                @block.vector
                def _(dve):
                    dve.memset(v_bd, 0.0).then_inc(v_zeroed, 1)
                    dve.memset(zeros[:], 0.0).then_inc(c_steps, 1)
                    dve.memset(k_st[:], 1.0).then_inc(all_copied, 1)
                    dve.wait_ge(c_exped, 1)
                    dve.tensor_scalar(c_one, c_exp, 1.0, None, ALU.add).then_inc(c_steps, 1)
                    dve.wait_ge(c_steps, 2)
                    dve.reciprocal(c_rec, c_one).then_inc(c_steps, 1)
                    dve.wait_ge(c_steps, 3)
                    dve.tensor_tensor(c_silu, c_t, c_rec, ALU.mult).then_inc(silu_ready, 1)
                    dve.wait_ge(mod_done, 1)
                    dve.tensor_copy(mod[:, 0:4, :], ps_m[0:B, :].rearrange("b (k d) -> b k d", d=D)).then_inc(mod_copied, 1)
                    dve.tensor_copy(mod[:, 4:6, :], ps_pv[0:B, 0:256].rearrange("b (k d) -> b k d", d=D)).then_inc(mod_copied, 1)
                    dve.wait_ge(mod_copied, 2)
                    for k in (1, 4):
                        dve.tensor_scalar(mod[:, k, :], mod[:, k, :], 1.0, None, ALU.add).then_inc(mod_ready, 1)
                    for n, k in enumerate((2, 5)):
                        dve.tensor_scalar(gate_sign[:, n, :], mod[:, k, :], 0.0, 2.0, ALU.is_ge, ALU.mult).then_inc(mod_steps, 1)
                        dve.tensor_scalar(gate_abs[:, n, :], mod[:, k, :], -1.0, 0.25, ALU.mult, ALU.max).then_inc(mod_steps, 1)
                    dve.wait_ge(mod_steps, 4)
                    for n, k in enumerate((2, 5)):
                        dve.tensor_tensor(gate_abs[:, n, :], gate_abs[:, n, :], mod[:, k, :], ALU.max).then_inc(mod_steps, 1)
                    dve.wait_ge(mod_steps, 6)
                    for n, k in enumerate((2, 5)):
                        dve.scalar_tensor_tensor(mod[:, k, :], gate_sign[:, n, :], -1.0, gate_abs[:, n, :],
                                                 ALU.add, ALU.mult).then_inc(mod_ready, 1)
                    dve.wait_ge(pairs_done, 1)
                    for m in range(3):
                        src = ps_s2[:, m, 0:D]
                        if m < 2:
                            dve.tensor_copy(w_qkv[:, m, :].rearrange("p (e h) -> p e h", h=HEADS),
                                            src.rearrange("p (h e) -> p e h", h=HEADS)).then_inc(all_copied, 1)
                        else:
                            dve.tensor_copy(w_qkv[:, m, :], src).then_inc(all_copied, 1)
                    dve.wait_ge(small_done, 1)
                    dve.tensor_copy(w_out[:], ps_s1[:, 0, 0:D]).then_inc(w_out_ready, 1)
                    dve.tensor_scalar(vb_wide, zeros[:], col("v_b"), None, ALU.add).then_inc(w_out_ready, 1)
                    dve.tensor_copy(w_fc1[:], ps_s1[:, 1, :]).then_inc(all_copied, 1)
                    dve.tensor_copy(w_fc2[:].rearrange("p k d -> p (k d)"), ps_s2[:, 3, :]).then_inc(all_copied, 1)
                    dve.wait_ge(bias_done, 1)
                    dve.tensor_tensor(out_bias[:], ps_m[:, 0:D], out_b_all, ALU.add).then_inc(all_copied, 1)

        def attend():
            xn = sb("xn", [P, NT, D], until=front)
            x_t = sb("x_t", [P, S], until=front)
            qk_f = sb("qk_f", [P, 2, S], until=front)
            qk_rest = sb("qk_rest", [P, 2, S], until=front)
            qk_part = sb("qk_part", [P, 2, 3, S], BF16, until=front)
            v_new = sb("v_new", [P, 2, S], until=front)
            row_max = sb("row_max", [P, 2, JH, NT], until=front)
            neg_max = sb("neg_max", [NT * JH, P], until=front)
            max_rest = sb("max_rest", [NT * JH, P], until=front)
            max_part = sb("max_part", [NT * JH, MROWS, P], BF16, until=front)
            ctx_raw = sb("ctx_raw", [P, 2, S], until=front)
            ctx_t = sb("ctx_t", [P, 2, S], until=front)
            ctx_n = sb("ctx_n", [P, S], until=front)
            sums = sb("sums", [P, HEADS * S // P], until=front)
            recs = sb("recs", [P, HEADS * S // P], until=front)
            rec_rows = sb("rec_rows", [HEADS, S], until=front)
            stats = sb("stats", [P, 2, NT, 6], until=front)
            moments = sb("moments", [P, 2, NT, 2], until=front)
            var_eps = sb("var_eps", [P, 2, NT], until=front)
            rstd = sb("rstd", [P, 2, NT], until=front)
            scaled = sb("scaled", [P, NT, D], until=front)

            probs = work[:].rearrange("p (b n) -> p b n", b=2)

            x_stats, x_moments, x_eps, x_rstd = sem("x_stats"), sem("x_moments"), sem("x_eps"), sem("x_rstd")
            x_scaled, h_ready, h_stats, h_moments = sem("x_scaled"), sem("h_ready"), sem("h_stats"), sem("h_moments")
            h_eps, h_rstd, xn_ready, h_biased = sem("h_eps"), sem("h_rstd"), sem("xn_ready"), sem("h_biased")
            filled = {u: sem("filled_" + u) for u in ("T", "Q", "K", "V", "M", "R", "O")}
            bank_emptied = sem("bank_emptied")
            qk_fp32 = sem("qk_fp32")
            qk_rest_ready, qk_mid, qk_low = sem("qk_rest_ready"), sem("qk_mid"), sem("qk_low")
            qk_stored, st_loaded = sem("qk_stored"), [sem(f"st_loaded{g}") for g in range(GROUPS)]
            max_fp32, max_rest_ready, max_mid, max_low = sem("max_fp32"), sem("max_rest_ready"), sem("max_mid"), sem("max_low")
            max_stored, max_loaded = sem("max_stored"), [sem(f"max_loaded{g}") for g in range(GROUPS)]
            s1_done, max_taken = sem("s1_done"), sem("max_taken")
            v_placed = sem("v_placed")
            s2_done, exp_done, pv_done = sem("s2_done"), sem("exp_done"), sem("pv_done")
            ctx_out, ctx_moved, sum_loaded = sem("ctx_out"), [sem("ctx_moved0"), sem("ctx_moved1")], sem("sum_loaded")
            rec_ready, rec_stored, rec_loaded, ctx_ready = sem("rec_ready"), sem("rec_stored"), sem("rec_loaded"), sem("ctx_ready")

            def half(st, lag):
                return 64 * (st.buffer(lag))

            with nc.Block() as block:
                @block.sync
                def _(sp):
                    def store_stack(st, m):
                        b = st.t + 2
                        loaded_before = worked_out(sp, 32 * (b - 1))
                        wait(sp, qk_low, 2 * b + m + 1)
                        for g in range(GROUPS):
                            wait(sp, st_loaded[g], loaded_before)
                        dst = (q_d, k_d)[m][st.buffer(2)].rearrange("k p s -> p k s")
                        part = qk_part[:, m]
                        if m == 0:
                            sp.dma_start(dst[:, 0:3], part[:, 0:3]).then_inc(qk_stored, 16)
                            sp.dma_start(dst[:, 3:5], part[:, 0:2]).then_inc(qk_stored, 16)
                            sp.dma_start(dst[:, 5:6], part[:, 0:1]).then_inc(qk_stored, 16)
                        else:
                            sp.dma_start(dst[:, 0:3], part[:, 0:1].to_broadcast([P, 3, S])).then_inc(qk_stored, 16)
                            sp.dma_start(dst[:, 3:5], part[:, 1:2].to_broadcast([P, 2, S])).then_inc(qk_stored, 16)
                            sp.dma_start(dst[:, 5:6], part[:, 2:3]).then_inc(qk_stored, 16)

                    def load_stack(st, lag, g):
                        b = st.t + lag
                        scores_done = worked_out(sp, NS2 * (GROUPS * (b - 2) + g + 1))
                        if g == 0:
                            wait(sp, qk_stored, 16 * 6 * (b + 1))
                        wait(sp, s2_done, scores_done)
                        lo = half(st, lag)
                        for dst, src in ((q_st, q_d), (k_st, k_d)):
                            rows = src[st.buffer(lag)].rearrange("k (e h) s -> (k e) h s", h=HEADS)
                            sp.dma_start(dst[lo:lo + SROWS, g:HEADS:GROUPS, :], rows[:, g:HEADS:GROUPS, :])\
                                .then_inc(st_loaded[g], 16)

                    def move_max(st, lag, g):
                        n = GROUPS * (st.t + lag) + g
                        stored_before = worked_out(sp, 16 * (st.t + lag))
                        wait(sp, max_low, n + 1)
                        wait(sp, max_loaded[g], stored_before)
                        sp.dma_start(max_d[g].rearrange("m j i s -> (j i) m s"), max_part[:]).then_inc(max_stored, 16)
                        wait(sp, max_stored, 16 * (n + 1))
                        lo = half(st, lag) + SROWS
                        sp.dma_start(q_st[lo:lo + MROWS, g:HEADS:GROUPS, :], max_d[g].rearrange("m j i s -> m j (i s)")).then_inc(max_loaded[g], 16)

                    def move_ctx(st, lag, g):
                        b = st.t + lag
                        n = GROUPS * b + g
                        wait(sp, ctx_out, n + 1)
                        if g == 0:
                            wait(sp, ctx_ready, b - 1)
                            wait(sp, sum_loaded, 16 * b)
                        for j in range(JH):
                            r = DH * (GROUPS * j + g)
                            sp.dma_start(ctx_t[r:r + DH, st.buffer(lag), :], ctx_raw[32 * j:32 * j + DH, g % 2, :])\
                                .then_inc(ctx_moved[g % 2], 16)
                        sp.dma_start(sum_d[g:HEADS:GROUPS, :], ctx_raw[DH:P:32, g % 2, :]).then_inc(ctx_moved[g % 2], 16)

                    def body(st):
                        t = st.t
                        if st.has(1):
                            load_stack(st, 1, 3)
                        if st.has(0):
                            move_max(st, 0, 3)
                        if st.has(-1):
                            move_ctx(st, -1, 3)
                            for half_of in ctx_moved:
                                wait(sp, half_of, 16 * (JH + 1) * GROUPS // 2 * t)
                            wait(sp, rec_ready, t - 1)
                            sp.dma_start(sums[:], sum_d.rearrange("h (c s) -> (h c) s", s=HEADS * S // P))\
                                .then_inc(sum_loaded, 16)
                        if st.has(2):
                            store_stack(st, 0)
                        if st.has(1):
                            move_max(st, 1, 0)
                        if st.has(-1):
                            stored_before = worked_out(sp, 16 * (t - 1))
                            wait(sp, rec_ready, t)
                            wait(sp, rec_loaded, stored_before)
                            sp.dma_start(rec_d.rearrange("h (c s) -> (h c) s", s=HEADS * S // P), recs[:])\
                                .then_inc(rec_stored, 16)
                            wait(sp, rec_stored, 16 * t)
                            wait(sp, filled["R"], t - 1)
                            sp.dma_start(rec_rows[:], rec_d).then_inc(rec_loaded, 16)
                        if st.has(2):
                            store_stack(st, 1)
                        if st.has(1):
                            move_max(st, 1, 1)
                        if st.has(0):
                            move_ctx(st, 0, 0)
                            move_ctx(st, 0, 1)
                        if st.has(1):
                            move_max(st, 1, 2)
                        if st.has(0):
                            move_ctx(st, 0, 2)
                        if st.has(2):
                            for g in range(GROUPS - 1):
                                load_stack(st, 2, g)

                    steps(sp, body)

                @block.gpsimd
                def _(pool):
                    def rstd_of(k, b, moments_ready, eps_added, ready):
                        wait(pool, moments_ready, NT * (b + 1))
                        pool.tensor_tensor(var_eps[:, k, :], moments[:, k, :, 1], ln_eps[:], ALU.add)\
                            .then_inc(eps_added, 1)
                        wait(pool, eps_added, b + 1)
                        pool.tensor_tensor(rstd[:, k, :], var_eps[:, k, :], half_neg[:], ALU.pow).then_inc(ready, 1)

                    def qk_remainder(st, m):
                        b = st.t + 2
                        wait(pool, qk_fp32, 2 * b + m + 1)
                        wait(pool, bank_emptied, st.number("QK"[m]) + 1)
                        wait(pool, qk_low, 2 * b + m)
                        pool.tensor_tensor(qk_rest[:, m], qk_f[:, m], qk_part[:, m, 0], ALU.subtract)\
                            .then_inc(qk_rest_ready, 1)

                    def qk_lowest(st, m):
                        b = st.t + 2
                        wait(pool, qk_mid, 2 * b + m + 1)
                        wait(pool, qk_rest_ready, 2 * b + m + 1)
                        pool.tensor_tensor(qk_part[:, m, 2], qk_rest[:, m], qk_part[:, m, 1], ALU.subtract)\
                            .then_inc(qk_low, 1)

                    def max_remainder(st, use, n):
                        wait(pool, max_fp32, n + 1)
                        wait(pool, bank_emptied, st.number(use) + 1)
                        pool.tensor_tensor(max_rest[:], neg_max[:], max_part[:, 0], ALU.subtract)\
                            .then_inc(max_rest_ready, 1)

                    def max_lowest(n):
                        wait(pool, max_mid, n + 1)
                        wait(pool, max_rest_ready, n + 1)
                        pool.tensor_tensor(max_part[:, 2], max_rest[:], max_part[:, 1], ALU.subtract)\
                            .then_inc(max_low, 1)

                    def body(st):
                        t = st.t
                        for g in range(GROUPS):
                            max_n = GROUPS * t + 3 if g == 0 else GROUPS * (t + 1) + g - 1
                            use = ("M3", "M0", "M1", "M2")[g]
                            if st.uses(use):
                                max_remainder(st, use, max_n)
                            if g == 0 and st.has(3):
                                rstd_of(0, t + 3, x_moments, x_eps, x_rstd)
                            if g == 1 and st.has(2):
                                qk_remainder(st, 0)
                            if g == 2 and st.has(2):
                                qk_remainder(st, 1)
                            if st.uses(use):
                                max_lowest(max_n)
                            if g == 1 and st.has(2):
                                qk_lowest(st, 0)
                            if g == 2 and st.has(2):
                                qk_lowest(st, 1)
                            if g == 1 and st.has(3):
                                rstd_of(1, t + 3, h_moments, h_eps, h_rstd)
                            if g == 3 and st.has(3):
                                wait(pool, xn_ready, NT * (t + 4))
                                hh = h_sb[:, bass.ds(NT * (t + 3), NT), :]
                                pool.tensor_tensor(hh, hh, out_bias[:].unsqueeze(1).to_broadcast([P, NT, D]), ALU.add)\
                                    .then_inc(h_biased, 1)

                    steps(pool, body)

                @block.scalar
                def _(act):
                    def exp_unit(st, g, u):
                        n = GROUPS * st.t + g
                        kt, js = S2_UNITS[u]
                        wait(act, s2_done, NS2 * n + u + 1)
                        if u == 0:
                            wait(act, pv_done, n - 1)
                        length = KT_LEN[kt]
                        cnt = len(js)
                        dst = probs[:, g % 2, KT_OFF[kt] + js[0] * length:KT_OFF[kt] + (js[0] + cnt) * length]
                        if kt < 2:
                            src = ps_s2[:, 2 * (u % 2):2 * (u % 2) + 2, 0:length]
                            dst = dst.rearrange("p (j s) -> p j s", j=cnt)
                        elif kt == 2:
                            src = ps_s2[:, 2 * (u % 2):2 * (u % 2) + 2, :]
                            dst = dst.rearrange("p (c s) -> p c s", c=2)
                        else:
                            src = ps_s2[:, 2 * (u % 2), :]
                        act.activation(dst, src, ACT.Exp, scale=SCALE).then_inc(exp_done, 1)

                    def empty_t(st):
                        b = st.t + 2
                        wait(act, filled["T"], b + 1)
                        wait(act, filled["V"], b)
                        act.activation(x_t[:], ps_m[:], ACT.Identity, bias=col("ln1_b"), scale=col("ln1_g"))\
                            .then_inc(bank_emptied, 1)

                    def empty_qk(st, m):
                        b = st.t + 2
                        wait(act, filled["QK"[m]], b + 1)
                        wait(act, qk_rest_ready, 2 * (b - 1) + m + 1)
                        act.activation(qk_f[:, m], ps_m[:], ACT.Identity, bias=col("qk"[m] + "_b")).then_inc(qk_fp32, 1)
                        wait(act, qk_stored, 16 * 6 * b)
                        act.activation(qk_part[:, m, 0], ps_m[:], ACT.Identity, bias=col("qk"[m] + "_b"))\
                            .then_inc(bank_emptied, 1)

                    def qk_middle(st, m):
                        b = st.t + 2
                        wait(act, qk_rest_ready, 2 * b + m + 1)
                        act.activation(qk_part[:, m, 1], qk_rest[:, m], ACT.Copy).then_inc(qk_mid, 1)

                    def empty_v(st):
                        b = st.t + 2
                        wait(act, filled["V"], b + 1)
                        wait(act, v_placed, b - 1)
                        act.activation(v_new[:, st.buffer(0), :], ps_m[:], ACT.Copy).then_inc(bank_emptied, 1)

                    def place_v(st):
                        wait(act, pv_done, GROUPS * st.t)
                        act.activation(v_sb[:, :, :, 0:DH].rearrange("p i h e -> p (i h) e"),
                                       v_new[:, st.buffer(0), :].rearrange("p (n e) -> p n e", e=DH), ACT.Copy)\
                            .then_inc(v_placed, 1)

                    def empty_max(n):
                        wait(act, filled["M"], n + 1)
                        wait(act, max_rest_ready, n)
                        act.activation(neg_max[:], ps_m[0:NT * JH, 0:P], ACT.Copy, scale=-1.0).then_inc(max_fp32, 1)
                        wait(act, max_stored, 16 * n)
                        act.activation(max_part[:, 0], ps_m[0:NT * JH, 0:P], ACT.Copy, scale=-1.0)\
                            .then_inc(bank_emptied, 1)

                    def max_middle(n):
                        wait(act, max_rest_ready, n + 1)
                        act.activation(max_part[:, 1], max_rest[:], ACT.Copy).then_inc(max_mid, 1)

                    def empty_ctx(b, g):
                        wait(act, pv_done, GROUPS * b + g + 1)
                        wait(act, ctx_moved[g % 2], 16 * (JH + 1) * (2 * b + g // 2))
                        act.activation(ctx_raw[:, g % 2, :], ps_pv[:], ACT.Copy).then_inc(ctx_out, 1)

                    def body(st):
                        t = st.t
                        for g in range(GROUPS):
                            max_n = GROUPS * t + 3 if g == 0 else GROUPS * (t + 1) + g - 1
                            use = ("M3", "M0", "M1", "M2")[g]
                            if st.has(0):
                                exp_unit(st, g, 0)
                                exp_unit(st, g, 1)
                            if st.has(2):
                                if g == 0:
                                    empty_t(st)
                                if g == 1:
                                    empty_qk(st, 1)
                                if g == 2:
                                    empty_v(st)
                            if st.has(0):
                                exp_unit(st, g, 2)
                            if g == 0 and st.has(-1):
                                empty_ctx(t - 1, 3)
                            elif g > 0 and st.has(0):
                                empty_ctx(t, g - 1)
                            if g == 0 and st.has(0):
                                place_v(st)
                            if st.has(0):
                                exp_unit(st, g, 3)
                            if st.uses(use):
                                empty_max(max_n)
                            if st.has(0):
                                exp_unit(st, g, 4)
                            if g == 0 and st.has(2):
                                empty_qk(st, 0)
                            if st.uses(use):
                                max_middle(max_n)
                            if g in (1, 2) and st.has(2):
                                qk_middle(st, g - 1)
                            if st.has(0):
                                exp_unit(st, g, 5)

                    steps(act, body)

                @block.tensor
                def _(pe):
                    def bank(st, use):
                        wait(pe, bank_emptied, st.number(use))

                    def transpose_x(st):
                        wait(pe, xn_ready, NT * (st.t + 3))
                        bank(st, "T")
                        for i in range(NT):
                            mm = pe.transpose(ps_m[:, i * P:(i + 1) * P], xn[:, i, :], ident[:])
                        mm.then_inc(filled["T"], 1)

                    def project(st, m):
                        bank(st, "QK"[m])
                        pe.matmul(ps_m[:], w_qkv[:, m, :], x_t[:], start=True, stop=True).then_inc(filled["QK"[m]], 1)

                    def project_v(st):
                        bank(st, "V")
                        for i in range(NT):
                            mm = pe.matmul(ps_m[:, i * P:(i + 1) * P], x_t[:, i * P:(i + 1) * P], w_qkv[:, 2, :],
                                           start=True, stop=True)
                        mm.then_inc(filled["V"], 1)

                    def s1_unit(st, g, u):
                        b = st.t + 1
                        i, js = S1_UNITS[u]
                        n = NS1 * (GROUPS * b + g) + u
                        if u == 0:
                            wait(pe, st_loaded[g], 32 * (b + 1))
                        wait(pe, max_taken, n - 1)
                        bnk = ps_s1[:, (NS1 * g + u) % 2, :]
                        keys = P * (i + 1)
                        diag = bnk[:, 0:len(js) * keys].rearrange("p (j s) -> p j s", j=len(js))[:, :, keys - P:keys]
                        pe.matmul(diag, ident_b[:], later_q[:, 0:len(js), :], start=True, stop=False,
                                  skip_group_check=True)
                        lo = half(st, 1)
                        for k, j in enumerate(js):
                            h = GROUPS * j + g
                            mm = pe.matmul(bnk[:, k * keys:(k + 1) * keys], q_st[lo:lo + SROWS, h, i * P:(i + 1) * P],
                                           k_st[lo:lo + SROWS, h, 0:keys], start=False, stop=True,
                                           skip_group_check=True)
                        mm.then_inc(s1_done, 1)

                    def transpose_max(st, use, n, g):
                        wait(pe, max_taken, NS1 * (n + 1))
                        bank(st, use)
                        if use == "M2" and st.has(-1):
                            wait(pe, ctx_ready, st.t)
                        pe.transpose(ps_m[0:NT * JH, 0:P], row_max[:, g % 2, :, :].rearrange("p j i -> p (j i)"),
                                     ident[:]).then_inc(filled["M"], 1)

                    def s2_unit(st, g, u):
                        n = GROUPS * st.t + g
                        kt, js = S2_UNITS[u]
                        if u == 0:
                            wait(pe, max_loaded[g], 16 * (st.t + 1))
                        wait(pe, exp_done, NS2 * n + u - 1)
                        lo = half(st, 0)
                        length = KT_LEN[kt]
                        per_bank = 512 // length
                        for k, j in enumerate(js):
                            h = GROUPS * j + g
                            bnk = ps_s2[:, 2 * (u % 2) + k // per_bank, :]
                            if k % per_bank == 0:
                                diag = bnk[:, 0:per_bank * length].rearrange("p (j s) -> p j s", j=per_bank)[:, :, 0:P]
                                pe.matmul(diag, ident_b[:], later_k[:, 0:per_bank, :], start=True, stop=False,
                                          skip_group_check=True)
                            dst = bnk[:, k % per_bank * length:(k % per_bank + 1) * length]
                            mm = pe.matmul(dst, k_st[lo:lo + SROWS + MROWS, h, kt * P:(kt + 1) * P],
                                           q_st[lo:lo + SROWS + MROWS, h, kt * P:S], start=False, stop=True,
                                           skip_group_check=True)
                        mm.then_inc(s2_done, 1)

                    def context(b, g):
                        n = GROUPS * b + g
                        wait(pe, exp_done, NS2 * (n + 1))
                        wait(pe, ctx_out, n)
                        if g == 0:
                            wait(pe, v_placed, b + 1)
                        for kt in range(NT):
                            for j in range(JH):
                                length = KT_LEN[kt]
                                at = KT_OFF[kt] + j * length
                                mm = pe.matmul(ps_pv[32 * j:32 * j + 32, kt * P:S], v_sb[:, kt, GROUPS * j + g, :],
                                               probs[:, g % 2, at:at + length], start=(kt == 0), stop=(kt == NT - 1),
                                               tile_position=(0, 32 * j))
                        mm.then_inc(pv_done, 1)

                    def spread_recs(st):
                        wait(pe, rec_loaded, 16 * st.t)
                        bank(st, "M2")
                        pe.matmul(ps_m[:], head_rows[:], rec_rows[:], start=True, stop=True).then_inc(filled["R"], 1)

                    def project_out(st):
                        wait(pe, ctx_ready, st.t)
                        bank(st, "O")
                        for i in range(NT):
                            mm = pe.matmul(ps_m[:, i * P:(i + 1) * P], ctx_n[:, i * P:(i + 1) * P], w_out[:],
                                           start=True, stop=True)
                        mm.then_inc(filled["O"], 1)

                    def body(st):
                        t = st.t
                        for g in range(GROUPS):
                            def s1(*us):
                                if st.has(1):
                                    for u in us:
                                        s1_unit(st, g, u)

                            def s2(u):
                                if st.has(0):
                                    s2_unit(st, g, u)
                            s2(0)
                            s1(0, 1)
                            s2(1)
                            s1(2, 3)
                            if st.has(2):
                                if g == 0:
                                    transpose_x(st)
                                if g == 1:
                                    project(st, 1)
                                if g == 2:
                                    project_v(st)
                            s2(2)
                            if g == 0 and st.has(-1):
                                context(t - 1, 3)
                            elif g > 0 and st.has(0):
                                context(t, g - 1)
                            s1(4, 5)
                            s2(3)
                            if g == 0 and st.has(0):
                                transpose_max(st, "M3", GROUPS * t + 3, 3)
                            elif g > 0 and st.has(1):
                                transpose_max(st, "M%d" % (g - 1), GROUPS * (t + 1) + g - 1, g - 1)
                            s1(6, 7)
                            s2(4)
                            s1(8)
                            if g == 0 and st.has(2):
                                project(st, 0)
                            if g == 2 and st.has(-1):
                                spread_recs(st)
                            if g == 3 and st.has(-1):
                                project_out(st)
                            s2(5)
                            s1(9, 10)

                    steps(pe, body)

                @block.vector
                def _(dve):
                    def tile_at(b, i):
                        return bass.ds(NT * b + i, 1)

                    def norm_stats(k, src, b, got, done):
                        for i in range(NT):
                            dve.bn_stats(stats[:, k, i, :], src(i)).then_inc(got, 1)
                        wait_apart(dve, got, NT * (b + 1), v_zeroed)
                        for i in range(NT):
                            dve.bn_aggr(moments[:, k, i, :], stats[:, k, i, :]).then_inc(done, 1)

                    def one(ap):
                        return ap.rearrange("p a d -> p (a d)")

                    def modulate(b):
                        wait(dve, x_rstd, b + 1)
                        for i in range(NT):
                            dve.scalar_tensor_tensor(scaled[:, i, :], one(x_sb[:, tile_at(b, i), :]),
                                                     moments[:, 0, i, 0:1], one(mod_sb[:, bass.ds(b, 1), D:2 * D]),
                                                     ALU.subtract, ALU.mult).then_inc(x_scaled, 1)
                        wait(dve, x_scaled, NT * (b + 1))
                        for i in range(NT):
                            dve.scalar_tensor_tensor(one(h_sb[:, tile_at(b, i), :]), scaled[:, i, :],
                                                     rstd[:, 0, i:i + 1], one(mod_sb[:, bass.ds(b, 1), 0:D]),
                                                     ALU.mult, ALU.add).then_inc(h_ready, 1)
                        wait_apart(dve, h_ready, NT * (b + 1), v_zeroed)
                        norm_stats(1, lambda i: one(h_sb[:, tile_at(b, i), :]), b, h_stats, h_moments)

                    def normalise(b):
                        wait(dve, h_rstd, b + 1)
                        wait(dve, filled["T"], b)
                        for i in range(NT):
                            dve.tensor_scalar(xn[:, i, :], one(h_sb[:, tile_at(b, i), :]), moments[:, 1, i, 0:1],
                                              rstd[:, 1, i:i + 1], ALU.subtract, ALU.mult).then_inc(xn_ready, 1)

                    def take_max(st, g, u):
                        n = GROUPS * (st.t + 1) + g
                        i, js = S1_UNITS[u]
                        wait(dve, s1_done, NS1 * n + u + 1)
                        if u == 0:
                            wait(dve, filled["M"], n - 1)
                        keys = P * (i + 1)
                        src = ps_s1[:, (NS1 * g + u) % 2, 0:len(js) * keys].rearrange("p (j s) -> p j s", j=len(js))
                        dve.reduce_max(row_max[:, g % 2, js[0]:js[0] + len(js), i], src, AXIS.X).then_inc(max_taken, 1)

                    def body(st):
                        t = st.t
                        for g in range(GROUPS):
                            for u in range(NS1):
                                if st.has(1):
                                    take_max(st, g, u)
                                if u == 3 and st.has(3):
                                    if g == 0:
                                        norm_stats(0, lambda i: one(x_sb[:, tile_at(t + 3, i), :]), t + 3,
                                                   x_stats, x_moments)
                                    if g == 1:
                                        modulate(t + 3)
                                    if g == 2:
                                        normalise(t + 3)
                                if u == 8 and st.has(-1) and g == 1:
                                    wait(dve, sum_loaded, 16 * t)
                                    wait(dve, rec_stored, 16 * (t - 1))
                                    dve.reciprocal(recs[:], sums[:]).then_inc(rec_ready, 1)
                                if u == 9 and st.has(-1):
                                    if g == 2:
                                        wait(dve, filled["R"], t)
                                        wait(dve, filled["O"], t - 1)
                                        for half_of in ctx_moved:
                                            wait(dve, half_of, 16 * (JH + 1) * GROUPS // 2 * t)
                                        dve.tensor_tensor(ctx_n[:], ctx_t[:, st.buffer(-1), :], ps_m[:], ALU.mult).then_inc(ctx_ready, 1)
                                    if g == 3:
                                        wait(dve, filled["O"], t)
                                        wait(dve, h_biased, t)
                                        hh = h_sb[:, bass.ds(NT * (t - 1), NT), :]
                                        dve.tensor_tensor(hh, ps_m[:].rearrange("p (i d) -> p i d", d=D), hh, ALU.add)\
                                            .then_inc(bank_emptied, 1)

                    steps(dve, body)

        def mlp():
            with ExitStack() as own:
                gates = sb("gates", [P, B, 4 * D], until=own)
                fc2_bias = sb("fc2_bias", [P, D], until=own)
                xn = sb("mlp_xn", [P, NT, D], until=own)
                x2_t = sb("x2_t", [P, S], until=own)
                hidden = sb("hidden", [P, NF, S], until=own)
                gated = sb("gated", [P, NT, D], until=own)
                scaled = sb("mlp_scaled", [P, NT, D], until=own)
                h3 = sb("h3", [P, NT, D], until=own)
                n3_tok = sb("n3_tok", [P, 2, NT, D], until=own)
                n3_new = sb("n3_new", [P, 2, S], until=own)
                stats = sb("mlp_stats", [P, 3, NT, 6], until=own)
                moments = sb("mlp_moments", [P, 3, NT, 2], until=own)
                var_eps = sb("mlp_var_eps", [P, 3, NT], until=own)
                mean_sq = sb("mean_sq", [P, NT], until=own)
                rstd = sb("mlp_rstd", [P, 3, NT], until=own)
                fill = sb("fill", [P, N_SLOTS // P, ROW], until=own)

                rows_loaded = sem("mlp_rows_loaded")
                got = [sem(f"mlp_stats{k}") for k in range(3)]
                have = [sem(f"mlp_moments{k}") for k in range(3)]
                eps_added = [sem(f"mlp_eps{k}") for k in range(3)]
                rstd_ready = [sem(f"mlp_rstd{k}") for k in range(3)]
                squared, square_mean = sem("squared"), sem("square_mean")
                xn_ready, h_biased = sem("mlp_xn_ready"), sem("mlp_h_biased")
                xt_done, xt_out, fc1_done, gelu_done = sem("xt_done"), sem("xt_out"), sem("fc1_done"), sem("gelu_done")
                fc2_done, summed, gate_done, x_done = sem("fc2_done"), sem("mlp_summed"), sem("gate_done"), sem("x_done")
                h3_scaled, h3_ready, n3_ready = sem("h3_scaled"), sem("h3_ready"), sem("n3_ready")
                n3t_done, n3t_out, n3t_moved = sem("n3t_done"), sem("n3t_out"), [sem("n3t_moved0"), sem("n3t_moved1")]
                n3_moved = [sem("n3_moved0"), sem("n3_moved1")]
                router_done, logits_out = sem("router_done"), sem("logits_out")
                zeroed, filled_in, slots_filled = sem("fill_zeroed"), sem("filled_in"), sem("slots_filled")

                def tile_of(tensor, b, i):
                    return tensor[:, bass.ds(NT * b + i, 1), :].rearrange("p a d -> p (a d)")

                def mlp_steps(eng, body):
                    pipeline(eng, body, -1, B, 2, 6)

                with nc.Block() as block:
                    @block.sync
                    def _(sp):
                        for k, at in enumerate((2, 3, 4, 5)):
                            sp.dma_start(gates[:, :, k * D:(k + 1) * D], mod_d[:, at * D:(at + 1) * D].partition_broadcast(P))\
                                .then_inc(rows_loaded, 16)
                        sp.dma_start(fc2_bias[:], a["fc2_b"].partition_broadcast(P)).then_inc(rows_loaded, 16)
                        sp.dma_start(router_t[:], a["router_t"]).then_inc(rows_loaded, 16)
                        sp.wait_ge(filled_in, 1)
                        sp.dma_start(slots_d.rearrange("(c p) w -> p c w", p=P), fill[:]).then_inc(slots_filled, 16)
                        sp.dma_start(shared_w1[:], a["sw1"]).then_inc(slots_filled, 16)
                        sp.dma_start(shared_w2[:], a["sw2"]).then_inc(slots_filled, 16)
                        sp.dma_start(eb2_all[:], a["eb2"].partition_broadcast(P)).then_inc(slots_filled, 16)
                        sp.dma_start(sb2_all[:], a["sb2"].partition_broadcast(P)).then_inc(slots_filled, 16)

                        def body(st):
                            if st.has(-1):
                                b = st.t - 1
                                wait_apart(sp, n3_ready, NT * (b + 1), v_zeroed)
                                sp.dma_start(n3x[:, bass.ds(NT * b, NT), 0:D], n3_tok[:, st.buffer(-1)]).then_inc(n3_moved[st.buffer(-1)], 16)
                                wait_apart(sp, n3t_out, b + 1, v_zeroed)
                                sp.dma_start(n3_t[:, bass.ds(S * b, S)], n3_new[:, st.buffer(-1), :]).then_inc(n3t_moved[st.buffer(-1)], 16)
                        mlp_steps(sp, body)
                        for moved in n3t_moved:
                            sp.wait_ge(moved, 16 * B // 2)
                        for moved in n3_moved:
                            sp.wait_ge(moved, 16 * B // 2)
                        sp.wait_ge(slots_filled, 16 * 5)

                    @block.gpsimd
                    def _(pool):
                        pool.memset(fill[:], 0.0).then_inc(zeroed, 1)
                        pool.wait_ge(zeroed, 1)
                        pool.iota(fill[:, :, D:D + 1].bitcast(I32), pattern=[[P, N_SLOTS // P], [0, 1]], base=2 * B * S,
                                  channel_multiplier=1).then_inc(filled_in, 1)
                        pool.iota(n3x[:, :, D:D + 1].bitcast(I32), pattern=[[P, B * NT], [0, 1]], base=0,
                                  channel_multiplier=1)
                        pool.memset(n3x[:, :, D + 1:ROW], 0.0)

                        def inverse_root(k, b, source, eps):
                            pool.tensor_tensor(var_eps[:, k, :], source, eps[:], ALU.add).then_inc(eps_added[k], 1)
                            pool.wait_ge(eps_added[k], b + 1)
                            pool.tensor_tensor(rstd[:, k, :], var_eps[:, k, :], half_neg[:], ALU.pow)\
                                .then_inc(rstd_ready[k], 1)

                        def body(st):
                            if st.has(1):
                                b = st.t + 1
                                pool.wait_ge(have[0], NT * (b + 1))
                                inverse_root(0, b, moments[:, 0, :, 1], ln_eps)
                                pool.wait_ge(xn_ready, NT * (b + 1))
                                hh = h_sb[:, bass.ds(NT * b, NT), :]
                                pool.tensor_tensor(hh, hh, fc2_bias[:].unsqueeze(1).to_broadcast([P, NT, D]), ALU.add)\
                                    .then_inc(h_biased, 1)
                            if st.has(0):
                                b = st.t
                                pool.wait_ge(have[1], NT * (b + 1))
                                inverse_root(1, b, moments[:, 1, :, 1], ln_eps)
                                pool.wait_ge(have[2], NT * (b + 1))
                                pool.tensor_tensor(mean_sq[:], moments[:, 2, :, 0], moments[:, 2, :, 0], ALU.mult)\
                                    .then_inc(squared, 1)
                                pool.wait_ge(squared, 2 * b + 1)
                                pool.tensor_tensor(mean_sq[:], mean_sq[:], moments[:, 2, :, 1], ALU.add)\
                                    .then_inc(squared, 1)
                                pool.wait_ge(squared, 2 * b + 2)
                                inverse_root(2, b, mean_sq[:], rms_eps)
                        pool.wait_ge(rows_loaded, 16 * 6)
                        mlp_steps(pool, body)

                    @block.scalar
                    def _(act):
                        def body(st):
                            if st.has(0):
                                b = st.t
                                act.wait_ge(xt_done, b + 1)
                                act.activation(x2_t[:], ps_m[:], ACT.Identity, bias=col("ln2_b"), scale=col("ln2_g"))\
                                    .then_inc(xt_out, 1)
                                for k in range(NF):
                                    act.wait_ge(fc1_done, NF * b + k + 1)
                                    if k == 0:
                                        wait(act, fc2_done, b)
                                    act.activation(hidden[:, k, :], ps_s2[:, k, :], ACT.Gelu_apprx_tanh,
                                                   bias=col("fc1_b", k)).then_inc(gelu_done, 1)
                            if st.has(-1):
                                b = st.t - 1
                                act.wait_ge(rstd_ready[2], b + 1)
                                wait(act, n3_moved[st.buffer(-1)], 8 * (b - st.buffer(-1)))
                                wait(act, n3t_done, b - 1)
                                for i in range(NT):
                                    act.activation(n3_tok[:, st.buffer(-1), i, :], h3[:, i, :], ACT.Copy, scale=rstd[:, 2, i:i + 1])\
                                        .then_inc(n3_ready, 1)
                                act.wait_ge(n3t_done, b + 1)
                                wait(act, n3t_moved[st.buffer(-1)], 8 * (b - st.buffer(-1)))
                                wait(act, router_done, b - 1)
                                act.activation(n3_new[:, st.buffer(-1), :], ps_s1[:, 0, :], ACT.Copy, scale=col("norm_w"))\
                                    .then_inc(n3t_out, 1)
                        mlp_steps(act, body)

                    @block.tensor
                    def _(pe):
                        def body(st):
                            if st.has(0):
                                b = st.t
                                pe.wait_ge(xn_ready, NT * (b + 1))
                                wait(pe, xt_out, b)
                                for i in range(NT):
                                    mm = pe.transpose(ps_m[:, i * P:(i + 1) * P], xn[:, i, :], ident[:])
                                mm.then_inc(xt_done, 1)
                                pe.wait_ge(xt_out, b + 1)
                                for k in range(NF):
                                    wait(pe, gelu_done, NF * (b - 1) + k + 1)
                                    pe.matmul(ps_s2[:, k, :], w_fc1[:, k * P:(k + 1) * P], x2_t[:], start=True, stop=True)\
                                        .then_inc(fc1_done, 1)
                            if st.has(-1):
                                b = st.t - 1
                                n3_of(pe, st, b)
                            if st.has(0):
                                b = st.t
                                pe.wait_ge(gelu_done, NF * (b + 1))
                                wait(pe, summed, b)
                                for i in range(NT):
                                    for k in range(NF):
                                        mm = pe.matmul(ps_pv[:, i * P:(i + 1) * P], hidden[:, k, i * P:(i + 1) * P],
                                                       w_fc2[:, k, :], start=(k == 0), stop=(k == NF - 1))
                                mm.then_inc(fc2_done, 1)

                        def n3_of(pe, st, b):
                            pe.wait_ge(n3_ready, NT * (b + 1))
                            wait(pe, n3t_out, b)
                            for i in range(NT):
                                mm = pe.transpose(ps_s1[:, 0, i * P:(i + 1) * P], n3_tok[:, st.buffer(-1), i, :], ident[:])
                            mm.then_inc(n3t_done, 1)
                            pe.wait_ge(n3t_out, b + 1)
                            wait(pe, logits_out, b)
                            for i in range(NT):
                                mm = pe.matmul(ps_s1[:, 1, i * E:(i + 1) * E], n3_new[:, st.buffer(-1), i * P:(i + 1) * P],
                                               router_t[:], start=True, stop=True)
                            mm.then_inc(router_done, 1)
                        pe.wait_ge(rows_loaded, 16 * 6)
                        mlp_steps(pe, body)

                    @block.vector
                    def _(dve):
                        def norm_stats(k, src, b):
                            for i in range(NT):
                                dve.bn_stats(stats[:, k, i, :], src(i)).then_inc(got[k], 1)
                            wait_apart(dve, got[k], NT * (b + 1), v_zeroed)
                            for i in range(NT):
                                dve.bn_aggr(moments[:, k, i, :], stats[:, k, i, :]).then_inc(have[k], 1)

                        def body(st):
                            if st.has(1):
                                b = st.t + 1
                                norm_stats(0, lambda i: tile_of(h_sb, b, i), b)
                                dve.wait_ge(rstd_ready[0], b + 1)
                                wait(dve, xt_done, b)
                                for i in range(NT):
                                    dve.tensor_scalar(xn[:, i, :], tile_of(h_sb, b, i), moments[:, 0, i, 0:1],
                                                      rstd[:, 0, i:i + 1], ALU.subtract, ALU.mult).then_inc(xn_ready, 1)
                            if st.has(-1):
                                b = st.t - 1
                                dve.wait_ge(router_done, b + 1)
                                dve.tensor_copy(logits[:, bass.ds(NT * b, NT), :],
                                                ps_s1[:, 1, 0:NT * E].rearrange("p (i e) -> p i e", e=E))\
                                    .then_inc(logits_out, 1)
                            if st.has(0):
                                b = st.t
                                x_all = x_sb[:, bass.ds(NT * b, NT), :]

                                def gate_row(k):
                                    return gates[:, bass.ds(b, 1), k * D:(k + 1) * D]
                                dve.wait_ge(fc2_done, b + 1)
                                dve.wait_ge(h_biased, b + 1)
                                dve.tensor_tensor(gated[:], ps_pv[:].rearrange("p (i d) -> p i d", d=D),
                                                  h_sb[:, bass.ds(NT * b, NT), :], ALU.add).then_inc(summed, 1)
                                dve.wait_ge(summed, b + 1)
                                dve.tensor_tensor(gated[:], gated[:], gate_row(0).to_broadcast([P, NT, D]), ALU.mult)\
                                    .then_inc(gate_done, 1)
                                dve.wait_ge(gate_done, b + 1)
                                dve.tensor_tensor(x_all, x_all, gated[:], ALU.add).then_inc(x_done, 1)
                                wait_apart(dve, x_done, b + 1, v_zeroed)
                                norm_stats(1, lambda i: tile_of(x_sb, b, i), b)
                                dve.wait_ge(rstd_ready[1], b + 1)
                                for i in range(NT):
                                    dve.scalar_tensor_tensor(scaled[:, i, :], tile_of(x_sb, b, i), moments[:, 1, i, 0:1],
                                                             gate_row(2).rearrange("p a d -> p (a d)"),
                                                             ALU.subtract, ALU.mult).then_inc(h3_scaled, 1)
                                dve.wait_ge(h3_scaled, NT * (b + 1))
                                wait(dve, n3_ready, NT * b)
                                for i in range(NT):
                                    dve.scalar_tensor_tensor(h3[:, i, :], scaled[:, i, :], rstd[:, 1, i:i + 1],
                                                             gate_row(1).rearrange("p a d -> p (a d)"),
                                                             ALU.mult, ALU.add).then_inc(h3_ready, 1)
                                dve.wait_ge(h3_ready, NT * (b + 1))
                                norm_stats(2, lambda i: h3[:, i, :], b)
                        dve.wait_ge(rows_loaded, 16 * 6)
                        mlp_steps(dve, body)

        def experts():
            with ExitStack() as own:
                w1 = sb("w1_all", [P, E, FF], until=own)
                w2 = sb("w2_all", [P, E, NF, D], until=own)
                eb2_rows = sb("eb2_rows", [E, D], until=own)
                gate_b = sb("gate_b", [P, B, D], until=own)
                sig = sb("sig", [P, B * NT, E], until=own)
                left = sb("left", [P, B * NT, E], until=own)
                comb = sb("comb", [P, B * NT, E], until=own)
                eq = sb("eq", [P, B * NT, E], until=own)
                rank = sb("rank", [P, E], until=own)
                pick = sb("pick", [P, 2, B * NT, E], until=own)
                best = sb("best", [P, 2, B * NT], until=own)
                rmax = sb("rmax", [P, B * NT], until=own)
                total = sb("total", [P, B * NT], until=own)
                comb_new = sb("comb_new", [P, NT, E], until=own)
                comb_t = sb("comb_t", [E, S], until=own)
                hidden = sb("e_hidden", [P, 2, NF, S], until=own)
                acc = sb("acc", [P, NT, D], until=own)
                result_b = sb("result_b", [P, 2, NT, D], until=own)
                w_in, exped, routing, route_done = sem("w_in"), sem("exped"), sem("routing"), sem("route_done")
                rank_ready = sem("rank_ready")
                comb_copied, comb_done, comb_out = sem("comb_copied"), sem("comb_done"), sem("comb_out")
                l1_done, relu_done, l2_done, acc_done = sem("l1_done"), sem("relu_done"), sem("l2_done"), sem("acc_done")
                bias_done2, final, stored = sem("bias_done2"), sem("final"), [sem("stored0"), sem("stored1")]
                NE = E + 1

                def e_steps(eng, body):
                    pipeline(eng, body, 0, B - 1, 2, B)

                with nc.Block() as block:
                    @block.sync
                    def _(sp):
                        sp.dma_start(w1[:], a["ew1"].rearrange("e p f -> p e f")).then_inc(w_in, 16)
                        sp.dma_start(w2[:].rearrange("p e k d -> p e (k d)"), a["ew2"].rearrange("e p k d -> p e (k d)")).then_inc(w_in, 16)
                        sp.dma_start(eb2_rows[:], a["eb2"]).then_inc(w_in, 16)
                        sp.dma_start(gate_b[:], mod_d[:, 5 * D:6 * D].partition_broadcast(P)).then_inc(w_in, 16)

                        def body(st):
                            b = st.t
                            wait_apart(sp, final, b + 1, v_zeroed)
                            sp.dma_start(out_tok[:, bass.ds(NT * b, NT), :], result_b[:, st.buffer(0)]).then_inc(stored[st.buffer(0)], 16)
                        e_steps(sp, body)
                        for half_stored in stored:
                            sp.wait_ge(half_stored, 16 * B // 2)

                    @block.gpsimd
                    def _(pool):
                        pool.iota(rank[:], pattern=[[-1, E]], base=E, channel_multiplier=0,
                                  allow_small_or_imprecise_dtypes=True).then_inc(rank_ready, 1)

                    @block.scalar
                    def _(act):
                        act.wait_ge(rank_ready, 2)
                        act.activation(sig[:], left[:], ACT.Exp, scale=-1.0).then_inc(exped, 1)

                        def body(st):
                            b = st.t
                            act.wait_ge(comb_done, b + 1)
                            act.activation(comb_t[:], ps_m[0:E, :], ACT.Copy).then_inc(comb_out, 1)
                            for e in range(NE):
                                n = NE * b + e
                                for k in range(NF):
                                    act.wait_ge(l1_done, NF * n + k + 1)
                                    if k == 0:
                                        wait(act, l2_done, n - 1)
                                    act.activation(hidden[:, (e + NE * st.phase) % 2, k, :], ps_s2[:, k, :], ACT.Relu,
                                                   bias=col("eb1", e * NF + k) if e < E else col("sb1", k)).then_inc(relu_done, 1)
                        e_steps(act, body)

                    @block.tensor
                    def _(pe):
                        pe.wait_ge(w_in, 64)

                        def layer1(b, e):
                            n = NE * b + e
                            for k in range(NF):
                                wait(pe, relu_done, NF * (n - 1) + k + 1)
                                w = w1[:, e, k * P:(k + 1) * P] if e < E else shared_w1[:, k * P:(k + 1) * P]
                                pe.matmul(ps_s2[:, k, :], w, n3_t[:, bass.ds(S * b, S)], start=True, stop=True).then_inc(l1_done, 1)

                        def body(st):
                            b = st.t
                            pe.wait_ge(comb_copied, b + 1)
                            for i in range(NT):
                                mm = pe.transpose(ps_m[0:E, i * P:(i + 1) * P], comb_new[:, i, :], ident[:])
                            mm.then_inc(comb_done, 1)
                            layer1(b, 0)
                            pe.wait_ge(comb_out, b + 1)
                            for i in range(NT):
                                mm = pe.matmul(ps_m[:, i * P:(i + 1) * P], comb_t[:, i * P:(i + 1) * P], eb2_rows[:], start=True, stop=True)
                            mm.then_inc(bias_done2, 1)
                            for e in range(NE):
                                n = NE * b + e
                                if e + 1 < NE:
                                    layer1(b, e + 1)
                                pe.wait_ge(relu_done, NF * (n + 1))
                                wait(pe, acc_done, n)
                                for i in range(NT):
                                    for k in range(NF):
                                        mm = pe.matmul(ps_pv[:, i * P:(i + 1) * P],
                                                       hidden[:, (e + NE * st.phase) % 2, k, i * P:(i + 1) * P],
                                                       w2[:, e, k, :] if e < E else shared_w2[:, k, :],
                                                       start=(k == 0), stop=(k == NF - 1))
                                mm.then_inc(l2_done, 1)
                        e_steps(pe, body)

                    @block.vector
                    def _(dve):
                        dve.tensor_scalar(left[:], logits[:], -80.0, None, ALU.max).then_inc(rank_ready, 1)
                        r = iter(range(1, 100))

                        def chain(op):
                            n = next(r)
                            op.then_inc(routing, 1)
                            dve.wait_ge(routing, n)
                        dve.wait_ge(exped, 1)
                        chain(dve.tensor_scalar(left[:], sig[:], 1.0, None, ALU.add))
                        chain(dve.reciprocal(sig[:], left[:]))
                        ranks = rank[:].unsqueeze(1).to_broadcast([P, B * NT, E])
                        src = sig
                        for c in range(2):
                            chain(dve.tensor_reduce(best[:, c], src[:], AXIS.X, ALU.max))
                            chain(dve.tensor_tensor(eq[:], src[:], best[:, c].unsqueeze(2).to_broadcast([P, B * NT, E]), ALU.is_equal))
                            chain(dve.tensor_tensor(eq[:], eq[:], ranks, ALU.mult))
                            chain(dve.tensor_reduce(rmax[:], eq[:], AXIS.X, ALU.max))
                            chain(dve.tensor_tensor(pick[:, c], eq[:], rmax[:].unsqueeze(2).to_broadcast([P, B * NT, E]), ALU.is_equal))
                            if c == 0:
                                chain(dve.scalar_tensor_tensor(left[:], pick[:, c], -4.0, sig[:], ALU.mult, ALU.add))
                                src = left
                        chain(dve.tensor_tensor(total[:], best[:, 0], best[:, 1], ALU.add))
                        chain(dve.tensor_scalar(total[:], total[:], 1e-6, None, ALU.add))
                        chain(dve.reciprocal(rmax[:], total[:]))
                        for c in range(2):
                            chain(dve.tensor_tensor(picked_w[:, c], best[:, c], rmax[:], ALU.mult))
                            chain(dve.tensor_tensor(pick[:, c], pick[:, c], picked_w[:, c].unsqueeze(2).to_broadcast([P, B * NT, E]), ALU.mult))
                        chain(dve.tensor_tensor(comb[:], pick[:, 0], pick[:, 1], ALU.add))

                        def body(st):
                            b = st.t
                            wait(dve, comb_done, b)
                            dve.tensor_copy(comb_new[:], comb[:, bass.ds(NT * b, NT), :]).then_inc(comb_copied, 1)
                            for e in range(NE):
                                n = NE * b + e
                                dve.wait_ge(l2_done, n + 1)
                                if e == 0:
                                    dve.wait_ge(bias_done2, b + 1)
                                    dve.wait_ge(comb_copied, b + 1)
                                    wait(dve, final, b)
                                    dve.tensor_copy(acc[:].rearrange("p i d -> p (i d)"), ps_m[:]).then_inc(final2, 1)
                                    dve.wait_ge(final2, 3 * b + 1)
                                for i in range(NT):
                                    op = dve.scalar_tensor_tensor(acc[:, i, :], ps_pv[:, i * P:(i + 1) * P],
                                                                  comb_new[:, i, e:e + 1] if e < E else 1.0,
                                                                  acc[:, i, :], ALU.mult, ALU.add)
                                op.then_inc(acc_done, 1)
                                dve.wait_ge(acc_done, n + 1)
                            wait(dve, stored[st.buffer(0)], 8 * (b - st.buffer(0)))
                            dve.tensor_tensor(acc[:], acc[:], sb2_all[:].unsqueeze(1).to_broadcast([P, NT, D]), ALU.add).then_inc(final2, 1)
                            dve.wait_ge(final2, 3 * b + 2)
                            dve.tensor_tensor(acc[:], acc[:], gate_b[:, bass.ds(b, 1), :].to_broadcast([P, NT, D]), ALU.mult).then_inc(final2, 1)
                            dve.wait_ge(final2, 3 * b + 3)
                            dve.tensor_tensor(result_b[:, st.buffer(0)], acc[:], x_sb[:, bass.ds(NT * b, NT), :], ALU.add).then_inc(final, 1)
                        final2 = sem("final2")
                        dve.wait_ge(w_in, 64)
                        e_steps(dve, body)

        setup()
        attend()
        front.close()
        router_t = sb("router_t", [P, E])
        logits = sb("logits", [P, B * NT, E])
        n3_t = sb("n3_t", [P, B * S])
        shared_w1 = sb("shared_w1", [P, FF])
        shared_w2 = sb("shared_w2", [P, NF, D])
        eb2_all = sb("eb2_all", [P, E, D])
        sb2_all = sb("sb2_all", [P, D])
        slots_d = dram("slots_d", (N_SLOTS, ROW))
        mlp()
        experts()


def kernel(**inputs):
    import numpy as np
    import concourse.bacc as bacc
    from concourse.bass_utils import run_bass_kernel_spmd

    g = {k[3:]: np.asarray(v) for k, v in inputs.items()}
    at = {k[5:]: v for k, v in g.items() if k.startswith("attn_")}
    ff = {k[4:]: v for k, v in g.items() if k.startswith("ffn_")}

    def heads_last(v):
        return v.T.reshape(-1, 1)

    def over_partitions(v, k):
        return v.reshape(k, P).T

    arrays = {
        "x": at["hidden_states"],
        "c_t": g["c"].T,
        "w_mod": g["wmod"],
        "u_t": np.stack([at[n + "_U"].reshape(D, PAIRS, 2 * RANK).transpose(2, 1, 0) for n in "qkv"], axis=1),
        "v_pairs": np.stack([at[n + "_V"].reshape(PAIRS, 2, RANK, DH).transpose(1, 2, 0, 3) for n in "qkv"], axis=2),
        "out_ut": at["out_U"].T,
        "out_v": at["out_V"],
        "fc1_ut": at["fc1_U"].T,
        "fc1_v": at["fc1_V"],
        "fc2_ut": at["fc2_U"].T,
        "fc2_v": at["fc2_V"],
        "out_b": at["out_b"],
        "fc2_b": at["fc2_b"],
        "sb2": ff["sb2"],
        "cols": np.concatenate([
            at["ln1_g"].reshape(P, 1), at["ln1_b"].reshape(P, 1), heads_last(at["q_b"]), heads_last(at["k_b"]),
            at["v_b"].reshape(P, 1), at["ln2_g"].reshape(P, 1), at["ln2_b"].reshape(P, 1),
            ff["norm_weight"].reshape(P, 1), over_partitions(at["fc1_b"], NF), over_partitions(ff["sb1"], NF),
            over_partitions(ff["eb1"], E * NF)], axis=1),
        "router_t": ff["router_w"].T,
        "sw1": ff["sw1"],
        "sw2": ff["sw2"].reshape(NF, P, D).transpose(1, 0, 2),
        "ew1": ff["ew1"],
        "ew2": ff["ew2"].reshape(E, NF, P, D).transpose(0, 2, 1, 3),
        "eb2": ff["eb2"],
    }
    nc = bacc.Bacc("TRN2", target_bir_lowering=False, num_devices=1)
    feed, aps = {}, {}
    for name, v in arrays.items():
        v = np.ascontiguousarray(v)
        feed["in_" + name] = v
        aps[name] = nc.dram_tensor("in_" + name, v.shape, mybir.dt.from_np(v.dtype), kind="ExternalInput").ap()
    result = nc.dram_tensor("result", (B, S, D), F32, kind="ExternalOutput").ap()
    adaln_block(nc, aps, result)
    r = run_bass_kernel_spmd(nc, [feed], core_ids=[0])
    return r.results[0]["result"]
```

```python
from contextlib import ExitStack

import concourse.bass as bass
from concourse import mybir

F32 = mybir.dt.float32
BF16 = mybir.dt.bfloat16
U32 = mybir.dt.uint32
I32 = mybir.dt.int32
ALU = mybir.AluOpType
ACT = mybir.ActivationFunctionType
AXIS = mybir.AxisListType

P = 128
B, S, D = 8, 512, 128
NT = S // P
HEADS, DH = 16, 8
RANK, PAIRS = 48, HEADS // 2
R_OUT, R_MLP = 96, 64
FF = 4 * D
NF = FF // P
E = 8
GROUPS, JH = 4, 4
PRODUCTS = [(0, 0), (0, 1), (0, 2), (1, 0), (1, 1), (2, 0)]
SROWS = DH * len(PRODUCTS)
MROWS = 3
MAX_ROW = 96
SCALE = float(DH) ** -0.5
LN_EPS, RMS_EPS = 1e-5, 1e-8
MASKED = -1e30

SLOTS = 256
N_TILES = (2 * B * S + E * (SLOTS - 1)) // SLOTS
N_SLOTS = N_TILES * SLOTS
EW = FF + NF * D + NF
ROW = D + 4

S1_UNITS = [(0, [0, 1, 2, 3]), (1, [0, 1]), (1, [2, 3])] + [(i, [j]) for i in (2, 3) for j in range(JH)]
S2_UNITS = [(0, [0, 1]), (0, [2, 3]), (1, [0, 1]), (1, [2, 3]), (2, [0, 1, 2, 3]), (3, [0, 1, 2, 3])]
NS1, NS2 = len(S1_UNITS), len(S2_UNITS)
KT_LEN = [S - P * k for k in range(NT)]
KT_OFF = [JH * sum(KT_LEN[:k]) for k in range(NT)]
PT_LEN = JH * sum(KT_LEN)

BANK_USES = ["T", "M3", "Q", "K", "M0", "V", "M1", "M2", "O"]
FIRST_STEP = -3


class Step:

    def __init__(self, t, phase, count=B):
        self.t, self.phase, self.count, self.steady = t, phase, count, not isinstance(t, int)

    def has(self, lag):
        return self.steady or 0 <= self.t + lag < self.count

    def first(self, lag):
        return not self.steady and self.t + lag == 0

    def buffer(self, lag, n=2):
        return (self.phase + lag) % n

    def uses(self, use):
        return self.has({"T": 2, "Q": 2, "K": 2, "V": 2, "M3": 0, "O": -1}.get(use, 1))

    def number(self, use):
        if self.steady:
            return (self.t - 1) * len(BANK_USES) + Step(1, 0).number(use)
        before = sum(Step(u, 0).uses(k) for u in range(FIRST_STEP, self.t) for k in BANK_USES)
        return before + sum(self.uses(k) for k in BANK_USES[:BANK_USES.index(use)])


def wait(eng, sem, value):
    if not isinstance(value, int) or value > 0:
        eng.wait_ge(sem, value)


def worked_out(eng, value):
    if not isinstance(value, int):
        eng.compute_val(value)
    return value


def wait_apart(eng, sem, value, done):
    value = worked_out(eng, value)
    eng.wait_ge(done, 1)
    wait(eng, sem, value)


def pipeline(eng, body, first, last, loop_from, loop_to, unroll=2, count=B):
    for t in range(first, loop_from):
        body(Step(t, t % unroll, count))
    with eng.Fori(loop_from, loop_to - unroll + 1, unroll) as t:
        for k in range(unroll):
            body(Step(t + k, (loop_from + k) % unroll, count))
    for t in range(loop_to, last + 1):
        body(Step(t, t % unroll, count))


def steps(eng, body):
    pipeline(eng, body, FIRST_STEP, B, 1, 5)

COLS = {}
N_COLS = 0
for _name, _n in (("ln1_g", 1), ("ln1_b", 1), ("q_b", 1), ("k_b", 1), ("v_b", 1), ("ln2_g", 1), ("ln2_b", 1),
                  ("norm_w", 1), ("fc1_b", NF), ("sb1", NF), ("eb1", E * NF)):
    COLS[_name] = N_COLS
    N_COLS += _n


def adaln_block(nc, a, out):
    ctx = ExitStack()
    with ctx:
        def sb(name, shape, dt=F32, until=ctx):
            return until.enter_context(nc.sbuf_tensor(name, shape, dt))

        def pb(name, shape):
            return ctx.enter_context(nc.psum_tensor(name, shape, F32))

        def sem(name):
            return ctx.enter_context(nc.semaphore(name))

        def dram(name, shape, dt=F32):
            return nc.dram_tensor(name, shape, dt, kind="Internal").ap()

        x_sb = sb("x_sb", [P, B * NT, D])
        h_sb = sb("h_sb", [P, B * NT, D])
        w_qkv = sb("w_qkv", [P, 3, D])
        w_out = sb("w_out", [P, D])
        w_fc1 = sb("w_fc1", [P, FF])
        w_fc2 = sb("w_fc2", [P, NF, D])
        cols = sb("cols", [P, N_COLS])
        out_bias = sb("out_bias", [P, D])
        ident = sb("ident", [P, P])
        ident_b = sb("ident_b", [P, P], BF16)
        later_q = sb("later_q", [P, JH, P], BF16)
        later_k = sb("later_k", [P, JH, P], BF16)
        head_rows = sb("head_rows", [HEADS, P])
        zeros = sb("zeros", [P, P])
        half_neg = sb("half_neg", [P, NT])
        ln_eps = sb("ln_eps", [P, NT])
        rms_eps = sb("rms_eps", [P, NT])
        per_d = sb("per_d", [P, NT])
        v_zeroed = sem("v_zeroed")
        slots = sb("slots", [P, 2, B * NT], U32)
        picked_w = sb("picked_w", [P, 2, B * NT])
        tile_expert = sb("tile_expert", [P, N_TILES], U32)

        front = ctx.enter_context(ExitStack())
        work = sb("work", [P, 2 * PT_LEN], until=front)

        q_st = [sb(f"q_st{k}", [P, HEADS, S], BF16, until=front) for k in range(2)]
        k_st = [sb(f"k_st{k}", [P, HEADS, S], BF16, until=front) for k in range(2)]
        v_sb = sb("v_sb", [P, NT, HEADS, 32], until=front)
        mod_sb = sb("mod_sb", [P, B, 2 * D], until=front)

        ps_s2 = pb("ps_s2", [P, 4, 512])
        ps_s1 = pb("ps_s1", [P, 2, 512])
        ps_pv = pb("ps_pv", [P, 512])
        ps_m = pb("ps_m", [P, 512])

        mod_d = dram("mod_d", (B, 6 * D))
        q_d = dram("q_d", (2, len(PRODUCTS), P, S), BF16)
        k_d = dram("k_d", (2, len(PRODUCTS), P, S), BF16)
        max_d = dram("max_d", (GROUPS, MROWS, JH, NT, P), BF16)
        sum_d = dram("sum_d", (HEADS, S))
        rec_d = dram("rec_d", (HEADS, S))

        out_tok = out.rearrange("b (i p) d -> p (b i) d", p=P)
        x_tok = a["x"].rearrange("b (i p) d -> p (b i) d", p=P)

        def col(name, k=0):
            return cols[:, COLS[name] + k:COLS[name] + k + 1]

        def setup():
            n_u = 3 * PAIRS * D
            u_t = work[0:2 * RANK, 0:n_u].rearrange("p (m k d) -> p m k d", m=3, k=PAIRS)
            at = n_u
            v_bd = work[0:2 * RANK, at:at + 3 * PAIRS * 16].rearrange("p (m k c) -> p m k c", m=3, k=PAIRS)
            at += 3 * PAIRS * 16
            out_ut = work[0:R_OUT, at:at + D]
            out_v = work[0:R_OUT, at + D:at + 2 * D]
            at += 2 * D
            fc1_ut = work[0:R_MLP, at:at + D]
            fc2_v = work[0:R_MLP, at + D:at + 2 * D]
            at += 2 * D
            fc1_v = work[0:R_MLP, at:at + FF]
            fc2_ut = work[0:R_MLP, at + FF:at + 2 * FF]
            at += 2 * FF
            w_mod = work[:, at:at + 6 * D]
            at += 6 * D
            mod = work[0:B, at:at + 6 * D].rearrange("b (k d) -> b k d", d=D)
            at += 6 * D
            vb_wide = work[:, at:at + D]
            out_b_all = work[:, at + D:at + 2 * D]
            at += 2 * D
            gate_sign = work[0:B, at:at + 2 * D].rearrange("b (k d) -> b k d", d=D)
            gate_abs = work[0:B, at + 2 * D:at + 4 * D].rearrange("b (k d) -> b k d", d=D)
            at += 4 * D
            c_t, c_exp, c_one, c_rec, c_silu = (work[:, at + B * k:at + B * (k + 1)] for k in range(5))

            c_loaded, w_loaded, x_loaded = sem("c_loaded"), sem("w_loaded"), sem("x_loaded")
            c_exped, c_steps, silu_ready = sem("c_exped"), sem("c_steps"), sem("silu_ready")
            mod_done, mod_copied, mod_steps, mod_ready = sem("mod_done"), sem("mod_copied"), sem("mod_steps"), sem("mod_ready")
            mod_stored, mod_spread, pairs_done, small_done = sem("mod_stored"), sem("mod_spread"), sem("pairs_done"), sem("small_done")
            w_out_ready, bias_done, consts, consts2 = sem("w_out_ready"), sem("bias_done"), sem("consts"), sem("consts2")
            all_copied = sem("all_copied")
            n_weight_loads = 2 + 6 + 1 + 6
            with nc.Block() as block:
                @block.sync
                def _(sp):
                    sp.dma_start(c_t, a["c_t"]).then_inc(c_loaded, 16)
                    sp.dma_start(w_mod, a["w_mod"]).then_inc(c_loaded, 16)
                    sp.dma_start(cols[:], a["cols"]).then_inc(w_loaded, 16)
                    sp.dma_start(u_t, a["u_t"]).then_inc(w_loaded, 16)
                    sp.wait_ge(v_zeroed, 1)
                    for hh in range(2):
                        for m in range(3):
                            sp.dma_start(v_bd[hh * RANK:(hh + 1) * RANK, m, :, hh * DH:(hh + 1) * DH],
                                         a["v_pairs"][hh, :, m]).then_inc(w_loaded, 16)
                    sp.dma_start(out_b_all, a["out_b"].partition_broadcast(P)).then_inc(w_loaded, 16)
                    for dst, name in ((out_ut, "out_ut"), (out_v, "out_v"), (fc1_ut, "fc1_ut"), (fc1_v, "fc1_v"),
                                      (fc2_ut, "fc2_ut"), (fc2_v, "fc2_v")):
                        sp.dma_start(dst, a[name]).then_inc(w_loaded, 16)
                    for b in range(B):
                        sp.dma_start(x_sb[:, NT * b:NT * (b + 1), :], x_tok[:, NT * b:NT * (b + 1), :])\
                            .then_inc(x_loaded, 16)
                    sp.wait_ge(mod_ready, 4)
                    sp.dma_start(mod_d, mod.rearrange("b k d -> b (k d)")).then_inc(mod_stored, 16)
                    sp.wait_ge(mod_stored, 16)
                    sp.dma_start(mod_sb[:], mod_d[:, 0:2 * D].partition_broadcast(P)).then_inc(mod_spread, 16)
                    sp.wait_ge(mod_spread, 16)
                    sp.wait_ge(x_loaded, 16 * B)

                @block.gpsimd
                def _(pool):
                    pool.memset(ident[:], 0.0).then_inc(consts, 1)
                    pool.memset(later_q[:], 0.0).then_inc(consts, 1)
                    pool.memset(later_k[:], 0.0).then_inc(consts, 1)
                    pool.memset(head_rows[:], 1.0).then_inc(consts, 1)
                    pool.memset(half_neg[:], -0.5).then_inc(consts, 1)
                    pool.memset(ln_eps[:], LN_EPS).then_inc(consts, 1)
                    pool.memset(rms_eps[:], RMS_EPS).then_inc(consts, 1)
                    pool.memset(per_d[:], 1.0 / D).then_inc(consts, 1)
                    pool.wait_ge(consts, 8)
                    pool.affine_select(out=ident[:], in_=ident[:], compare_op=ALU.not_equal, fill=1.0, base=0,
                                       pattern=[[-1, P]], channel_multiplier=1).then_inc(consts2, 1)
                    pool.affine_select(out=later_q[:], in_=later_q[:], compare_op=ALU.is_ge, fill=MASKED, base=0,
                                       pattern=[[0, JH], [-1, P]], channel_multiplier=1).then_inc(consts2, 1)
                    pool.affine_select(out=later_k[:], in_=later_k[:], compare_op=ALU.is_ge, fill=MASKED, base=0,
                                       pattern=[[0, JH], [1, P]], channel_multiplier=-1).then_inc(consts2, 1)
                    pool.affine_select(out=head_rows[:], in_=head_rows[:], compare_op=ALU.is_ge, fill=0.0, base=0,
                                       pattern=[[1, P]], channel_multiplier=-DH).then_inc(consts2, 1)
                    pool.wait_ge(consts2, 4)
                    pool.affine_select(out=head_rows[:], in_=head_rows[:], compare_op=ALU.is_ge, fill=0.0,
                                       base=DH - 1, pattern=[[-1, P]], channel_multiplier=DH).then_inc(consts2, 1)
                    pool.tensor_copy(ident_b[:], ident[:]).then_inc(consts2, 1)
                    pool.memset(v_sb[:], 1.0).then_inc(consts2, 1)
                    for k in range(2):
                        pool.memset(k_st[k][:].bitcast(F32), 0.0).then_inc(consts2, 1)
                    pool.wait_ge(consts2, 9)
                    for k in range(2):
                        pool.memset(k_st[k][MAX_ROW:P], 1.0)

                @block.scalar
                def _(act):
                    act.wait_ge(c_loaded, 32)
                    act.activation(c_exp, c_t, ACT.Exp, scale=-1.0).then_inc(c_exped, 1)
                    act.wait_ge(c_steps, 1)
                    for stack in q_st:
                        act.activation(stack[0:MAX_ROW], zeros[0:MAX_ROW, 0:1].unsqueeze(1).to_broadcast([MAX_ROW, HEADS, S]),
                                       ACT.Copy)

                @block.tensor
                def _(pe):
                    pe.wait_ge(silu_ready, 1)
                    pe.matmul(ps_m[0:B, :], c_silu, w_mod[:, 0:512], start=True, stop=True)
                    pe.matmul(ps_pv[0:B, 0:256], c_silu, w_mod[:, 512:768], start=True, stop=True).then_inc(mod_done, 1)
                    pe.wait_ge(w_loaded, 16 * n_weight_loads)
                    for m in range(3):
                        for k in range(PAIRS):
                            mm = pe.matmul(ps_s2[:, m, 16 * k:16 * k + 16], u_t[:, m, k, :], v_bd[:, m, k, :],
                                           start=True, stop=True)
                    mm.then_inc(pairs_done, 1)
                    pe.matmul(ps_s1[:, 0, 0:D], out_ut, out_v, start=True, stop=True)
                    pe.matmul(ps_s1[:, 1, :], fc1_ut, fc1_v, start=True, stop=True)
                    for k in range(NF):
                        mm = pe.matmul(ps_s2[:, 3, k * P:(k + 1) * P], fc2_ut[:, k * P:(k + 1) * P], fc2_v,
                                       start=True, stop=True)
                    mm.then_inc(small_done, 1)
                    pe.wait_ge(w_out_ready, 2)
                    pe.wait_ge(mod_copied, 2)
                    pe.matmul(ps_m[:, 0:D], vb_wide, w_out[:], start=True, stop=True).then_inc(bias_done, 1)

                @block.vector
                def _(dve):
                    dve.memset(v_bd, 0.0).then_inc(v_zeroed, 1)
                    dve.memset(zeros[:], 0.0).then_inc(c_steps, 1)
                    dve.wait_ge(c_exped, 1)
                    dve.tensor_scalar(c_one, c_exp, 1.0, None, ALU.add).then_inc(c_steps, 1)
                    dve.wait_ge(c_steps, 2)
                    dve.reciprocal(c_rec, c_one).then_inc(c_steps, 1)
                    dve.wait_ge(c_steps, 3)
                    dve.tensor_tensor(c_silu, c_t, c_rec, ALU.mult).then_inc(silu_ready, 1)
                    dve.wait_ge(mod_done, 1)
                    dve.tensor_copy(mod[:, 0:4, :], ps_m[0:B, :].rearrange("b (k d) -> b k d", d=D)).then_inc(mod_copied, 1)
                    dve.tensor_copy(mod[:, 4:6, :], ps_pv[0:B, 0:256].rearrange("b (k d) -> b k d", d=D)).then_inc(mod_copied, 1)
                    dve.wait_ge(mod_copied, 2)
                    for k in (1, 4):
                        dve.tensor_scalar(mod[:, k, :], mod[:, k, :], 1.0, None, ALU.add).then_inc(mod_ready, 1)
                    for n, k in enumerate((2, 5)):
                        dve.tensor_scalar(gate_sign[:, n, :], mod[:, k, :], 0.0, 2.0, ALU.is_ge, ALU.mult).then_inc(mod_steps, 1)
                        dve.tensor_scalar(gate_abs[:, n, :], mod[:, k, :], -1.0, 0.25, ALU.mult, ALU.max).then_inc(mod_steps, 1)
                    dve.wait_ge(mod_steps, 4)
                    for n, k in enumerate((2, 5)):
                        dve.tensor_tensor(gate_abs[:, n, :], gate_abs[:, n, :], mod[:, k, :], ALU.max).then_inc(mod_steps, 1)
                    dve.wait_ge(mod_steps, 6)
                    for n, k in enumerate((2, 5)):
                        dve.scalar_tensor_tensor(mod[:, k, :], gate_sign[:, n, :], -1.0, gate_abs[:, n, :],
                                                 ALU.add, ALU.mult).then_inc(mod_ready, 1)
                    dve.wait_ge(pairs_done, 1)
                    for m in range(3):
                        src = ps_s2[:, m, 0:D]
                        if m < 2:
                            dve.tensor_copy(w_qkv[:, m, :].rearrange("p (e h) -> p e h", h=HEADS),
                                            src.rearrange("p (h e) -> p e h", h=HEADS)).then_inc(all_copied, 1)
                        else:
                            dve.tensor_copy(w_qkv[:, m, :], src).then_inc(all_copied, 1)
                    dve.wait_ge(small_done, 1)
                    dve.tensor_copy(w_out[:], ps_s1[:, 0, 0:D]).then_inc(w_out_ready, 1)
                    dve.tensor_scalar(vb_wide, zeros[:], col("v_b"), None, ALU.add).then_inc(w_out_ready, 1)
                    dve.tensor_copy(w_fc1[:], ps_s1[:, 1, :]).then_inc(all_copied, 1)
                    dve.tensor_copy(w_fc2[:].rearrange("p k d -> p (k d)"), ps_s2[:, 3, :]).then_inc(all_copied, 1)
                    dve.wait_ge(bias_done, 1)
                    dve.tensor_tensor(out_bias[:], ps_m[:, 0:D], out_b_all, ALU.add).then_inc(all_copied, 1)

        def attend():
            xn = sb("xn", [P, NT, D], until=front)
            x_t = sb("x_t", [P, S], until=front)
            qk_f = sb("qk_f", [P, 2, S], until=front)
            qk_rest = sb("qk_rest", [P, 2, S], until=front)
            qk_part = sb("qk_part", [P, 2, 3, S], BF16, until=front)
            v_new = sb("v_new", [P, 2, S], until=front)
            row_max = sb("row_max", [P, 2, JH, NT], until=front)
            neg_max = sb("neg_max", [NT * JH, P], until=front)
            max_rest = sb("max_rest", [NT * JH, P], until=front)
            max_part = sb("max_part", [NT * JH, MROWS, P], BF16, until=front)
            ctx_raw = sb("ctx_raw", [P, 2, S], until=front)
            ctx_t = sb("ctx_t", [P, 2, S], until=front)
            ctx_n = sb("ctx_n", [P, S], until=front)
            sums = sb("sums", [P, HEADS * S // P], until=front)
            recs = sb("recs", [P, HEADS * S // P], until=front)
            rec_rows = sb("rec_rows", [HEADS, S], until=front)
            stats = sb("stats", [P, 2, NT, 6], until=front)
            moments = sb("moments", [P, 2, NT, 2], until=front)
            var_eps = sb("var_eps", [P, 2, NT], until=front)
            rstd = sb("rstd", [P, 2, NT], until=front)
            scaled = sb("scaled", [P, NT, D], until=front)

            probs = work[:].rearrange("p (b n) -> p b n", b=2)

            x_stats, x_moments, x_eps, x_rstd = sem("x_stats"), sem("x_moments"), sem("x_eps"), sem("x_rstd")
            x_scaled, h_ready, h_stats, h_moments = sem("x_scaled"), sem("h_ready"), sem("h_stats"), sem("h_moments")
            h_eps, h_rstd, xn_ready, h_biased = sem("h_eps"), sem("h_rstd"), sem("xn_ready"), sem("h_biased")
            filled = {u: sem("filled_" + u) for u in ("T", "Q", "K", "V", "M", "R", "O")}
            bank_emptied = sem("bank_emptied")
            qk_fp32 = sem("qk_fp32")
            qk_rest_ready, qk_mid, qk_low = sem("qk_rest_ready"), sem("qk_mid"), sem("qk_low")
            qk_stored, st_loaded = sem("qk_stored"), [sem(f"st_loaded{g}") for g in range(GROUPS)]
            max_fp32, max_rest_ready, max_mid, max_low = sem("max_fp32"), sem("max_rest_ready"), sem("max_mid"), sem("max_low")
            max_stored, max_loaded = sem("max_stored"), [sem(f"max_loaded{g}") for g in range(GROUPS)]
            s1_done, max_taken = sem("s1_done"), sem("max_taken")
            v_placed = sem("v_placed")
            s2_done, exp_done, pv_done = sem("s2_done"), sem("exp_done"), sem("pv_done")
            ctx_out, ctx_moved, sum_loaded = sem("ctx_out"), [sem("ctx_moved0"), sem("ctx_moved1")], sem("sum_loaded")
            rec_ready, rec_stored, rec_loaded, ctx_ready = sem("rec_ready"), sem("rec_stored"), sem("rec_loaded"), sem("ctx_ready")

            with nc.Block() as block:
                @block.sync
                def _(sp):
                    def store_stack(st, m):
                        b = st.t + 2
                        loaded_before = worked_out(sp, 32 * (b - 1))
                        wait(sp, qk_low, 2 * b + m + 1)
                        for g in range(GROUPS):
                            wait(sp, st_loaded[g], loaded_before)
                        dst = (q_d, k_d)[m][st.buffer(2)].rearrange("k p s -> p k s")
                        part = qk_part[:, m]
                        if m == 0:
                            sp.dma_start(dst[:, 0:3], part[:, 0:3]).then_inc(qk_stored, 16)
                            sp.dma_start(dst[:, 3:5], part[:, 0:2]).then_inc(qk_stored, 16)
                            sp.dma_start(dst[:, 5:6], part[:, 0:1]).then_inc(qk_stored, 16)
                        else:
                            sp.dma_start(dst[:, 0:3], part[:, 0:1].to_broadcast([P, 3, S])).then_inc(qk_stored, 16)
                            sp.dma_start(dst[:, 3:5], part[:, 1:2].to_broadcast([P, 2, S])).then_inc(qk_stored, 16)
                            sp.dma_start(dst[:, 5:6], part[:, 2:3]).then_inc(qk_stored, 16)

                    def load_stack(st, lag, g):
                        b = st.t + lag
                        scores_done = worked_out(sp, NS2 * (GROUPS * (b - 2) + g + 1))
                        if g == 0:
                            wait(sp, qk_stored, 16 * 6 * (b + 1))
                        wait(sp, s2_done, scores_done)
                        for dst, src in ((q_st, q_d), (k_st, k_d)):
                            rows = src[st.buffer(lag)].rearrange("k (e h) s -> (k e) h s", h=HEADS)
                            sp.dma_start(dst[st.buffer(lag)][0:SROWS, g:HEADS:GROUPS, :], rows[:, g:HEADS:GROUPS, :])\
                                .then_inc(st_loaded[g], 16)

                    def move_max(st, lag, g):
                        n = GROUPS * (st.t + lag) + g
                        stored_before = worked_out(sp, 16 * (st.t + lag))
                        wait(sp, max_low, n + 1)
                        wait(sp, max_loaded[g], stored_before)
                        sp.dma_start(max_d[g].rearrange("m j i s -> (j i) m s"), max_part[:]).then_inc(max_stored, 16)
                        wait(sp, max_stored, 16 * (n + 1))
                        sp.dma_start(q_st[st.buffer(lag)][MAX_ROW:MAX_ROW + MROWS, g:HEADS:GROUPS, :], max_d[g].rearrange("m j i s -> m j (i s)")).then_inc(max_loaded[g], 16)

                    def move_ctx(st, lag, g):
                        b = st.t + lag
                        n = GROUPS * b + g
                        wait(sp, ctx_out, n + 1)
                        if g == 0:
                            wait(sp, ctx_ready, b - 1)
                            wait(sp, sum_loaded, 16 * b)
                        for j in range(JH):
                            r = DH * (GROUPS * j + g)
                            sp.dma_start(ctx_t[r:r + DH, st.buffer(lag), :], ctx_raw[32 * j:32 * j + DH, g % 2, :])\
                                .then_inc(ctx_moved[g % 2], 16)
                        sp.dma_start(sum_d[g:HEADS:GROUPS, :], ctx_raw[DH:P:32, g % 2, :]).then_inc(ctx_moved[g % 2], 16)

                    def body(st):
                        t = st.t
                        if st.has(1):
                            load_stack(st, 1, 3)
                        if st.has(-1):
                            move_ctx(st, -1, 3)
                        if st.has(0):
                            move_max(st, 0, 3)
                        if st.has(-1):
                            for half_of in ctx_moved:
                                wait(sp, half_of, 16 * (JH + 1) * GROUPS // 2 * t)
                            wait(sp, rec_ready, t - 1)
                            sp.dma_start(sums[:], sum_d.rearrange("h (c s) -> (h c) s", s=HEADS * S // P))\
                                .then_inc(sum_loaded, 16)
                        if st.has(2):
                            store_stack(st, 0)
                        if st.has(-1):
                            stored_before = worked_out(sp, 16 * (t - 1))
                            wait(sp, rec_ready, t)
                            wait(sp, rec_loaded, stored_before)
                            sp.dma_start(rec_d.rearrange("h (c s) -> (h c) s", s=HEADS * S // P), recs[:])\
                                .then_inc(rec_stored, 16)
                        if st.has(0):
                            move_ctx(st, 0, 0)
                        if st.has(-1):
                            wait(sp, rec_stored, 16 * t)
                            wait(sp, filled["R"], t - 1)
                            sp.dma_start(rec_rows[:], rec_d).then_inc(rec_loaded, 16)
                        if st.has(1):
                            move_max(st, 1, 0)
                        if st.has(2):
                            store_stack(st, 1)
                            load_stack(st, 2, 0)
                            load_stack(st, 2, 1)
                        if st.has(0):
                            move_ctx(st, 0, 1)
                        if st.has(1):
                            move_max(st, 1, 1)
                        if st.has(2):
                            load_stack(st, 2, 2)
                        if st.has(0):
                            move_ctx(st, 0, 2)
                        if st.has(1):
                            move_max(st, 1, 2)

                    steps(sp, body)

                @block.gpsimd
                def _(pool):
                    def rstd_of(k, b, moments_ready, eps_added, ready):
                        wait(pool, moments_ready, NT * (b + 1))
                        pool.tensor_tensor(var_eps[:, k, :], moments[:, k, :, 1], ln_eps[:], ALU.add)\
                            .then_inc(eps_added, 1)
                        wait(pool, eps_added, b + 1)
                        pool.tensor_tensor(rstd[:, k, :], var_eps[:, k, :], half_neg[:], ALU.pow).then_inc(ready, 1)

                    def qk_remainder(st, m):
                        b = st.t + 2
                        wait(pool, qk_fp32, 2 * b + m + 1)
                        wait(pool, bank_emptied, st.number("QK"[m]) + 1)
                        wait(pool, qk_low, 2 * b + m)
                        pool.tensor_tensor(qk_rest[:, m], qk_f[:, m], qk_part[:, m, 0], ALU.subtract)\
                            .then_inc(qk_rest_ready, 1)

                    def qk_lowest(st, m):
                        b = st.t + 2
                        wait(pool, qk_mid, 2 * b + m + 1)
                        wait(pool, qk_rest_ready, 2 * b + m + 1)
                        pool.tensor_tensor(qk_part[:, m, 2], qk_rest[:, m], qk_part[:, m, 1], ALU.subtract)\
                            .then_inc(qk_low, 1)

                    def max_remainder(st, use, n):
                        wait(pool, max_fp32, n + 1)
                        wait(pool, bank_emptied, st.number(use) + 1)
                        pool.tensor_tensor(max_rest[:], neg_max[:], max_part[:, 0], ALU.subtract)\
                            .then_inc(max_rest_ready, 1)

                    def max_lowest(n):
                        wait(pool, max_mid, n + 1)
                        wait(pool, max_rest_ready, n + 1)
                        pool.tensor_tensor(max_part[:, 2], max_rest[:], max_part[:, 1], ALU.subtract)\
                            .then_inc(max_low, 1)

                    def body(st):
                        t = st.t
                        for g in range(GROUPS):
                            max_n = GROUPS * t + 3 if g == 0 else GROUPS * (t + 1) + g - 1
                            use = ("M3", "M0", "M1", "M2")[g]
                            if g == 2 and st.has(2):
                                qk_lowest(st, 1)
                            if st.uses(use):
                                max_remainder(st, use, max_n)
                            if g == 0 and st.has(3):
                                rstd_of(0, t + 3, x_moments, x_eps, x_rstd)
                            if g == 1 and st.has(2):
                                qk_remainder(st, 0)
                            if st.uses(use):
                                max_lowest(max_n)
                            if g == 1 and st.has(2):
                                qk_lowest(st, 0)
                                qk_remainder(st, 1)
                            if g == 1 and st.has(3):
                                rstd_of(1, t + 3, h_moments, h_eps, h_rstd)
                            if g == 3 and st.has(3):
                                wait(pool, xn_ready, NT * (t + 4))
                                hh = h_sb[:, bass.ds(NT * (t + 3), NT), :]
                                pool.tensor_tensor(hh, hh, out_bias[:].unsqueeze(1).to_broadcast([P, NT, D]), ALU.add)\
                                    .then_inc(h_biased, 1)

                    steps(pool, body)

                @block.scalar
                def _(act):
                    def exp_unit(st, g, u):
                        n = GROUPS * st.t + g
                        kt, js = S2_UNITS[u]
                        wait(act, s2_done, NS2 * n + u + 1)
                        if u == 0:
                            wait(act, pv_done, n - 1)
                        length = KT_LEN[kt]
                        cnt = len(js)
                        dst = probs[:, g % 2, KT_OFF[kt] + js[0] * length:KT_OFF[kt] + (js[0] + cnt) * length]
                        if kt < 2:
                            src = ps_s2[:, 2 * (u % 2):2 * (u % 2) + 2, 0:length]
                            dst = dst.rearrange("p (j s) -> p j s", j=cnt)
                        elif kt == 2:
                            src = ps_s2[:, 2 * (u % 2):2 * (u % 2) + 2, :]
                            dst = dst.rearrange("p (c s) -> p c s", c=2)
                        else:
                            src = ps_s2[:, 2 * (u % 2), :]
                        act.activation(dst, src, ACT.Exp, scale=SCALE).then_inc(exp_done, 1)

                    def empty_t(st):
                        b = st.t + 2
                        wait(act, filled["T"], b + 1)
                        wait(act, filled["V"], b)
                        act.activation(x_t[:], ps_m[:], ACT.Identity, bias=col("ln1_b"), scale=col("ln1_g"))\
                            .then_inc(bank_emptied, 1)

                    def empty_qk(st, m):
                        b = st.t + 2
                        wait(act, filled["QK"[m]], b + 1)
                        wait(act, qk_rest_ready, 2 * (b - 1) + m + 1)
                        act.activation(qk_f[:, m], ps_m[:], ACT.Identity, bias=col("qk"[m] + "_b")).then_inc(qk_fp32, 1)
                        wait(act, qk_stored, 16 * 6 * b)
                        act.activation(qk_part[:, m, 0], ps_m[:], ACT.Identity, bias=col("qk"[m] + "_b"))\
                            .then_inc(bank_emptied, 1)

                    def qk_middle(st, m):
                        b = st.t + 2
                        wait(act, qk_rest_ready, 2 * b + m + 1)
                        act.activation(qk_part[:, m, 1], qk_rest[:, m], ACT.Copy).then_inc(qk_mid, 1)

                    def empty_v(st):
                        b = st.t + 2
                        wait(act, filled["V"], b + 1)
                        wait(act, v_placed, b - 1)
                        act.activation(v_new[:, st.buffer(0), :], ps_m[:], ACT.Copy).then_inc(bank_emptied, 1)

                    def place_v(st):
                        wait(act, pv_done, GROUPS * st.t)
                        act.activation(v_sb[:, :, :, 0:DH].rearrange("p i h e -> p (i h) e"),
                                       v_new[:, st.buffer(0), :].rearrange("p (n e) -> p n e", e=DH), ACT.Copy)\
                            .then_inc(v_placed, 1)

                    def empty_max(n):
                        wait(act, filled["M"], n + 1)
                        wait(act, max_rest_ready, n)
                        act.activation(neg_max[:], ps_m[0:NT * JH, 0:P], ACT.Copy, scale=-1.0).then_inc(max_fp32, 1)
                        wait(act, max_stored, 16 * n)
                        act.activation(max_part[:, 0], ps_m[0:NT * JH, 0:P], ACT.Copy, scale=-1.0)\
                            .then_inc(bank_emptied, 1)

                    def max_middle(n):
                        wait(act, max_rest_ready, n + 1)
                        act.activation(max_part[:, 1], max_rest[:], ACT.Copy).then_inc(max_mid, 1)

                    def empty_ctx(b, g):
                        wait(act, pv_done, GROUPS * b + g + 1)
                        wait(act, ctx_moved[g % 2], 16 * (JH + 1) * (2 * b + g // 2))
                        act.activation(ctx_raw[:, g % 2, :], ps_pv[:], ACT.Copy).then_inc(ctx_out, 1)

                    def body(st):
                        t = st.t
                        for g in range(GROUPS):
                            max_n = GROUPS * t + 3 if g == 0 else GROUPS * (t + 1) + g - 1
                            use = ("M3", "M0", "M1", "M2")[g]
                            if st.has(0):
                                exp_unit(st, g, 0)
                                exp_unit(st, g, 1)
                            if st.has(2):
                                if g == 0:
                                    empty_t(st)
                                if g == 1:
                                    empty_qk(st, 1)
                                if g == 2:
                                    qk_middle(st, 1)
                                    empty_v(st)
                            if st.has(0):
                                exp_unit(st, g, 2)
                            if g == 0 and st.has(-1):
                                empty_ctx(t - 1, 3)
                            elif g > 0 and st.has(0):
                                empty_ctx(t, g - 1)
                            if g == 0 and st.has(0):
                                place_v(st)
                            if st.has(0):
                                exp_unit(st, g, 3)
                            if st.uses(use):
                                empty_max(max_n)
                            if st.has(0):
                                exp_unit(st, g, 4)
                            if g == 0 and st.has(2):
                                empty_qk(st, 0)
                            if st.uses(use):
                                max_middle(max_n)
                            if g == 1 and st.has(2):
                                qk_middle(st, 0)
                            if st.has(0):
                                exp_unit(st, g, 5)

                    steps(act, body)

                @block.tensor
                def _(pe):
                    def bank(st, use):
                        wait(pe, bank_emptied, st.number(use))

                    def transpose_x(st):
                        wait(pe, xn_ready, NT * (st.t + 3))
                        bank(st, "T")
                        for i in range(NT):
                            mm = pe.transpose(ps_m[:, i * P:(i + 1) * P], xn[:, i, :], ident[:])
                        mm.then_inc(filled["T"], 1)

                    def project(st, m):
                        bank(st, "QK"[m])
                        pe.matmul(ps_m[:], w_qkv[:, m, :], x_t[:], start=True, stop=True).then_inc(filled["QK"[m]], 1)

                    def project_v(st):
                        bank(st, "V")
                        for i in range(NT):
                            mm = pe.matmul(ps_m[:, i * P:(i + 1) * P], x_t[:, i * P:(i + 1) * P], w_qkv[:, 2, :],
                                           start=True, stop=True)
                        mm.then_inc(filled["V"], 1)

                    def s1_unit(st, g, u):
                        b = st.t + 1
                        i, js = S1_UNITS[u]
                        n = NS1 * (GROUPS * b + g) + u
                        if u == 0:
                            wait(pe, st_loaded[g], 32 * (b + 1))
                        wait(pe, max_taken, n - 1)
                        bnk = ps_s1[:, (NS1 * g + u) % 2, :]
                        keys = P * (i + 1)
                        diag = bnk[:, 0:len(js) * keys].rearrange("p (j s) -> p j s", j=len(js))[:, :, keys - P:keys]
                        pe.matmul(diag, ident_b[:], later_q[:, 0:len(js), :], start=True, stop=False,
                                  skip_group_check=True)
                        q, keys_of = q_st[st.buffer(1)], k_st[st.buffer(1)]
                        for k, j in enumerate(js):
                            h = GROUPS * j + g
                            mm = pe.matmul(bnk[:, k * keys:(k + 1) * keys], q[0:MAX_ROW, h, i * P:(i + 1) * P],
                                           keys_of[0:MAX_ROW, h, 0:keys], start=False, stop=True,
                                           skip_group_check=True)
                        mm.then_inc(s1_done, 1)

                    def transpose_max(st, use, n, g):
                        wait(pe, max_taken, NS1 * (n + 1))
                        bank(st, use)
                        if use == "M2" and st.has(-1):
                            wait(pe, ctx_ready, st.t)
                        pe.transpose(ps_m[0:NT * JH, 0:P], row_max[:, g % 2, :, :].rearrange("p j i -> p (j i)"),
                                     ident[:]).then_inc(filled["M"], 1)

                    def s2_unit(st, g, u):
                        n = GROUPS * st.t + g
                        kt, js = S2_UNITS[u]
                        if u == 0:
                            wait(pe, max_loaded[g], 16 * (st.t + 1))
                        wait(pe, exp_done, NS2 * n + u - 1)
                        q, keys_of = q_st[st.buffer(0)], k_st[st.buffer(0)]
                        length = KT_LEN[kt]
                        per_bank = 512 // length
                        for k, j in enumerate(js):
                            h = GROUPS * j + g
                            bnk = ps_s2[:, 2 * (u % 2) + k // per_bank, :]
                            if k % per_bank == 0:
                                diag = bnk[:, 0:per_bank * length].rearrange("p (j s) -> p j s", j=per_bank)[:, :, 0:P]
                                pe.matmul(diag, ident_b[:], later_k[:, 0:per_bank, :], start=True, stop=False,
                                          skip_group_check=True)
                            dst = bnk[:, k % per_bank * length:(k % per_bank + 1) * length]
                            mm = pe.matmul(dst, keys_of[0:MAX_ROW + MROWS, h, kt * P:(kt + 1) * P],
                                           q[0:MAX_ROW + MROWS, h, kt * P:S], start=False, stop=True,
                                           skip_group_check=True)
                        mm.then_inc(s2_done, 1)

                    def context(b, g):
                        n = GROUPS * b + g
                        wait(pe, exp_done, NS2 * (n + 1))
                        wait(pe, ctx_out, n)
                        if g == 0:
                            wait(pe, v_placed, b + 1)
                        for kt in range(NT):
                            for j in range(JH):
                                length = KT_LEN[kt]
                                at = KT_OFF[kt] + j * length
                                mm = pe.matmul(ps_pv[32 * j:32 * j + 32, kt * P:S], v_sb[:, kt, GROUPS * j + g, :],
                                               probs[:, g % 2, at:at + length], start=(kt == 0), stop=(kt == NT - 1),
                                               tile_position=(0, 32 * j))
                        mm.then_inc(pv_done, 1)

                    def spread_recs(st):
                        wait(pe, rec_loaded, 16 * st.t)
                        bank(st, "M2")
                        pe.matmul(ps_m[:], head_rows[:], rec_rows[:], start=True, stop=True).then_inc(filled["R"], 1)

                    def project_out(st):
                        wait(pe, ctx_ready, st.t)
                        bank(st, "O")
                        for i in range(NT):
                            mm = pe.matmul(ps_m[:, i * P:(i + 1) * P], ctx_n[:, i * P:(i + 1) * P], w_out[:],
                                           start=True, stop=True)
                        mm.then_inc(filled["O"], 1)

                    def body(st):
                        t = st.t
                        for g in range(GROUPS):
                            def s1(*us):
                                if st.has(1):
                                    for u in us:
                                        s1_unit(st, g, u)

                            def s2(u):
                                if st.has(0):
                                    s2_unit(st, g, u)
                            s2(0)
                            s1(0, 1)
                            s2(1)
                            s1(2, 3)
                            if st.has(2):
                                if g == 0:
                                    transpose_x(st)
                                if g == 1:
                                    project(st, 1)
                                if g == 2:
                                    project_v(st)
                            s2(2)
                            if g == 0 and st.has(-1):
                                context(t - 1, 3)
                            elif g > 0 and st.has(0):
                                context(t, g - 1)
                            s1(4, 5)
                            s2(3)
                            if g == 0 and st.has(0):
                                transpose_max(st, "M3", GROUPS * t + 3, 3)
                            elif g > 0 and st.has(1):
                                transpose_max(st, "M%d" % (g - 1), GROUPS * (t + 1) + g - 1, g - 1)
                            s1(6, 7)
                            s2(4)
                            s1(8)
                            if g == 0 and st.has(2):
                                project(st, 0)
                            if g == 2 and st.has(-1):
                                spread_recs(st)
                            s2(5)
                            s1(9, 10)
                            if g == 3 and st.has(-1):
                                project_out(st)

                    steps(pe, body)

                @block.vector
                def _(dve):
                    def tile_at(b, i):
                        return bass.ds(NT * b + i, 1)

                    def norm_stats(k, src, b, got, done):
                        for i in range(NT):
                            dve.bn_stats(stats[:, k, i, :], src(i)).then_inc(got, 1)
                        wait_apart(dve, got, NT * (b + 1), v_zeroed)
                        for i in range(NT):
                            dve.bn_aggr(moments[:, k, i, :], stats[:, k, i, :]).then_inc(done, 1)

                    def one(ap):
                        return ap.rearrange("p a d -> p (a d)")

                    def scale_x(b):
                        wait(dve, x_rstd, b + 1)
                        for i in range(NT):
                            dve.scalar_tensor_tensor(scaled[:, i, :], one(x_sb[:, tile_at(b, i), :]),
                                                     moments[:, 0, i, 0:1], one(mod_sb[:, bass.ds(b, 1), D:2 * D]),
                                                     ALU.subtract, ALU.mult).then_inc(x_scaled, 1)

                    def shift_x(b):
                        wait(dve, x_scaled, NT * (b + 1))
                        for i in range(NT):
                            dve.scalar_tensor_tensor(one(h_sb[:, tile_at(b, i), :]), scaled[:, i, :],
                                                     rstd[:, 0, i:i + 1], one(mod_sb[:, bass.ds(b, 1), 0:D]),
                                                     ALU.mult, ALU.add).then_inc(h_ready, 1)

                    def h_norm_stats(b):
                        wait_apart(dve, h_ready, NT * (b + 1), v_zeroed)
                        norm_stats(1, lambda i: one(h_sb[:, tile_at(b, i), :]), b, h_stats, h_moments)

                    def normalise(b):
                        wait(dve, h_rstd, b + 1)
                        wait(dve, filled["T"], b)
                        for i in range(NT):
                            dve.tensor_scalar(xn[:, i, :], one(h_sb[:, tile_at(b, i), :]), moments[:, 1, i, 0:1],
                                              rstd[:, 1, i:i + 1], ALU.subtract, ALU.mult).then_inc(xn_ready, 1)

                    def take_max(st, g, u):
                        n = GROUPS * (st.t + 1) + g
                        i, js = S1_UNITS[u]
                        wait(dve, s1_done, NS1 * n + u + 1)
                        if u == 0:
                            wait(dve, filled["M"], n - 1)
                        keys = P * (i + 1)
                        src = ps_s1[:, (NS1 * g + u) % 2, 0:len(js) * keys].rearrange("p (j s) -> p j s", j=len(js))
                        dve.reduce_max(row_max[:, g % 2, js[0]:js[0] + len(js), i], src, AXIS.X).then_inc(max_taken, 1)

                    def body(st):
                        t = st.t
                        for g in range(GROUPS):
                            for u in range(NS1):
                                if st.has(1):
                                    take_max(st, g, u)
                                if st.has(3):
                                    if (g, u) == (0, 3):
                                        norm_stats(0, lambda i: one(x_sb[:, tile_at(t + 3, i), :]), t + 3,
                                                   x_stats, x_moments)
                                    if (g, u) == (1, 1):
                                        scale_x(t + 3)
                                    if (g, u) == (1, 3):
                                        shift_x(t + 3)
                                    if (g, u) == (1, 6):
                                        h_norm_stats(t + 3)
                                    if (g, u) == (2, 3):
                                        normalise(t + 3)
                                if u == 8 and st.has(-1) and g == 1:
                                    wait(dve, sum_loaded, 16 * t)
                                    wait(dve, rec_stored, 16 * (t - 1))
                                    dve.reciprocal(recs[:], sums[:]).then_inc(rec_ready, 1)
                                if u == (9 if g == 2 else 10) and st.has(-1):
                                    if g == 2:
                                        wait(dve, filled["R"], t)
                                        wait(dve, filled["O"], t - 1)
                                        for half_of in ctx_moved:
                                            wait(dve, half_of, 16 * (JH + 1) * GROUPS // 2 * t)
                                        dve.tensor_tensor(ctx_n[:], ctx_t[:, st.buffer(-1), :], ps_m[:], ALU.mult).then_inc(ctx_ready, 1)
                                    if g == 3:
                                        wait(dve, filled["O"], t)
                                        wait(dve, h_biased, t)
                                        hh = h_sb[:, bass.ds(NT * (t - 1), NT), :]
                                        dve.tensor_tensor(hh, ps_m[:].rearrange("p (i d) -> p i d", d=D), hh, ALU.add)\
                                            .then_inc(bank_emptied, 1)

                    steps(dve, body)

        def mlp():
            with ExitStack() as own:
                gates = sb("gates", [P, B, 4 * D], until=own)
                fc2_bias = sb("fc2_bias", [P, D], until=own)
                xn = sb("mlp_xn", [P, 2, NT, D], until=own)
                x2_t = sb("x2_t", [P, S], until=own)
                hidden = sb("hidden", [P, NF, S], until=own)
                gated = sb("gated", [P, NT, D], until=own)
                scaled = sb("mlp_scaled", [P, NT, D], until=own)
                h3 = sb("h3", [P, 2, NT, D], until=own)
                n3_tok = sb("n3_tok", [P, 2, NT, D], until=own)
                n3_new = sb("n3_new", [P, 2, S], until=own)
                stats = sb("mlp_stats", [P, 3, 2, NT, 6], until=own)
                moments = sb("mlp_moments", [P, 3, 2, NT, 2], until=own)
                var_eps = sb("mlp_var_eps", [P, 3, 2, NT], until=own)
                square = sb("square", [P, D], until=own)
                sum_sq = sb("sum_sq", [P, 2, NT], until=own)
                mean_sq = sb("mean_sq", [P, NT], until=own)
                rstd = sb("mlp_rstd", [P, 3, 2, NT], until=own)
                fill = sb("fill", [P, N_SLOTS // P, ROW], until=own)

                rows_loaded = sem("mlp_rows_loaded")
                got = [sem(f"mlp_stats{k}") for k in range(3)]
                have = [sem(f"mlp_moments{k}") for k in range(3)]
                eps_added = [sem(f"mlp_eps{k}") for k in range(3)]
                rstd_ready = [sem(f"mlp_rstd{k}") for k in range(3)]
                squared, averaged = sem("squared"), sem("averaged")
                xn_ready, h_biased = sem("mlp_xn_ready"), sem("mlp_h_biased")
                xt_done, xt_out, fc1_done, gelu_done = sem("xt_done"), sem("xt_out"), sem("fc1_done"), sem("gelu_done")
                fc2_done, summed, gate_done, x_done = sem("fc2_done"), sem("mlp_summed"), sem("gate_done"), sem("x_done")
                h3_scaled, h3_ready, n3_ready = sem("h3_scaled"), sem("h3_ready"), sem("n3_ready")
                n3t_done, n3t_out, n3t_moved = sem("n3t_done"), sem("n3t_out"), [sem("n3t_moved0"), sem("n3t_moved1")]
                n3_moved = [sem("n3_moved0"), sem("n3_moved1")]
                router_done, logits_out = sem("router_done"), sem("logits_out")
                zeroed, filled_in, slots_filled = sem("fill_zeroed"), sem("filled_in"), sem("slots_filled")

                def tile_of(tensor, b, i):
                    return tensor[:, bass.ds(NT * b + i, 1), :].rearrange("p a d -> p (a d)")

                def mlp_steps(eng, body):
                    pipeline(eng, body, -2, B + 1, 2, 6)

                with nc.Block() as block:
                    @block.sync
                    def _(sp):
                        for k, at in enumerate((2, 3, 4, 5)):
                            sp.dma_start(gates[:, :, k * D:(k + 1) * D], mod_d[:, at * D:(at + 1) * D].partition_broadcast(P))\
                                .then_inc(rows_loaded, 16)
                        sp.dma_start(fc2_bias[:], a["fc2_b"].partition_broadcast(P)).then_inc(rows_loaded, 16)
                        sp.dma_start(router_t[:], a["router_t"]).then_inc(rows_loaded, 16)
                        sp.wait_ge(filled_in, 1)
                        sp.wait_ge(zeroed, 1)
                        sp.dma_start(slots_d.rearrange("(c p) w -> p c w", p=P), fill[:]).then_inc(slots_filled, 16)
                        sp.dma_start(shared_w1[:], a["sw1"]).then_inc(slots_filled, 16)
                        sp.dma_start(shared_w2[:], a["sw2"]).then_inc(slots_filled, 16)
                        sp.dma_start(sb2_all[:], a["sb2"].partition_broadcast(P)).then_inc(slots_filled, 16)

                        def body(st):
                            if st.has(-2):
                                b = st.t - 2
                                wait_apart(sp, n3_ready, NT * (b + 1), v_zeroed)
                                sp.dma_start(n3x[:, bass.ds(NT * b, NT), 0:D], n3_tok[:, st.buffer(-2)]).then_inc(n3_moved[st.buffer(-2)], 16)
                                wait_apart(sp, n3t_out, b + 1, v_zeroed)
                                sp.dma_start(n3_t[:, bass.ds(S * b, S)], n3_new[:, st.buffer(-2), :]).then_inc(n3t_moved[st.buffer(-2)], 16)
                        mlp_steps(sp, body)
                        for moved in n3t_moved:
                            sp.wait_ge(moved, 16 * B // 2)
                        for moved in n3_moved:
                            sp.wait_ge(moved, 16 * B // 2)
                        sp.wait_ge(slots_filled, 16 * 4)

                    @block.gpsimd
                    def _(pool):
                        pool.memset(fill[:, :, D + 1:ROW], 0.0)
                        pool.iota(fill[:, :, D:D + 1].bitcast(I32), pattern=[[P, N_SLOTS // P], [0, 1]], base=2 * B * S,
                                  channel_multiplier=1).then_inc(filled_in, 1)
                        pool.iota(n3x[:, :, D:D + 1].bitcast(I32), pattern=[[P, B * NT], [0, 1]], base=0,
                                  channel_multiplier=1)
                        pool.memset(n3x[:, :, D + 1:ROW], 0.0)

                        def inverse_root(k, b, m, source, eps):
                            pool.tensor_tensor(var_eps[:, k, m, :], source, eps[:], ALU.add).then_inc(eps_added[k], 1)
                            pool.wait_ge(eps_added[k], b + 1)
                            pool.tensor_tensor(rstd[:, k, m, :], var_eps[:, k, m, :], half_neg[:], ALU.pow)\
                                .then_inc(rstd_ready[k], 1)

                        def body(st):
                            if st.has(1):
                                b = st.t + 1
                                if st.first(1):
                                    pool.wait_ge(rows_loaded, 16 * 6)
                                pool.wait_ge(xn_ready, NT * (b + 1))
                                hh = h_sb[:, bass.ds(NT * b, NT), :]
                                pool.tensor_tensor(hh, hh, fc2_bias[:].unsqueeze(1).to_broadcast([P, NT, D]), ALU.add)\
                                    .then_inc(h_biased, 1)
                            if st.has(-1):
                                b, m = st.t - 1, st.buffer(-1)
                                pool.wait_ge(squared, NT * (b + 1))
                                wait(pool, rstd_ready[2], b)
                                pool.tensor_tensor(mean_sq[:], sum_sq[:, m, :], per_d[:], ALU.mult)\
                                    .then_inc(averaged, 1)
                                pool.wait_ge(averaged, b + 1)
                                wait(pool, n3_ready, NT * (b - 1))
                                inverse_root(2, b, m, mean_sq[:], rms_eps)
                            if st.has(2):
                                b, m = st.t + 2, st.buffer(2)
                                pool.wait_ge(have[0], NT * (b + 1))
                                inverse_root(0, b, m, moments[:, 0, m, :, 1], ln_eps)
                            if st.has(0):
                                b, m = st.t, st.buffer(0)
                                pool.wait_ge(have[1], NT * (b + 1))
                                inverse_root(1, b, m, moments[:, 1, m, :, 1], ln_eps)
                        mlp_steps(pool, body)

                    @block.scalar
                    def _(act):
                        act.activation(fill[:, :, 0:D], zeros[:].unsqueeze(1).to_broadcast([P, N_SLOTS // P, D]), ACT.Copy)\
                            .then_inc(zeroed, 1)

                        def body(st):
                            if st.has(-2):
                                b, m = st.t - 2, st.buffer(-2)
                                act.wait_ge(rstd_ready[2], b + 1)
                                wait(act, n3_moved[m], 8 * (b - m))
                                for i in range(NT):
                                    act.activation(n3_tok[:, m, i, :], h3[:, m, i, :], ACT.Copy, scale=rstd[:, 2, m, i:i + 1])\
                                        .then_inc(n3_ready, 1)
                            if st.has(0):
                                b = st.t
                                for k in range(NF):
                                    act.wait_ge(fc1_done, NF * b + k + 1)
                                    if k == 0:
                                        wait(act, fc2_done, b)
                                    act.activation(hidden[:, k, :], ps_s2[:, k, :], ACT.Gelu_apprx_tanh,
                                                   bias=col("fc1_b", k)).then_inc(gelu_done, 1)
                            if st.has(1):
                                b = st.t + 1
                                act.wait_ge(xt_done, b + 1)
                                act.activation(x2_t[:], ps_m[:], ACT.Identity, bias=col("ln2_b"), scale=col("ln2_g"))\
                                    .then_inc(xt_out, 1)
                            if st.has(-1):
                                b, m = st.t - 1, st.buffer(-1)
                                for i in range(NT):
                                    act.wait_ge(h3_ready, NT * b + i + 1)
                                    wait(act, squared, NT * b + i)
                                    act.activation(square[:], h3[:, m, i, :], ACT.Square,
                                                   accum_out=sum_sq[:, m, i:i + 1]).then_inc(squared, 1)
                            if st.has(-2):
                                act.wait_ge(n3t_done, st.t - 1)
                                m = st.buffer(-2)
                                wait(act, n3t_moved[m], 8 * (st.t - 2 - m))
                                act.activation(n3_new[:, m, :], ps_s1[:, 0, :], ACT.Copy, scale=col("norm_w"))\
                                    .then_inc(n3t_out, 1)
                        mlp_steps(act, body)

                    @block.tensor
                    def _(pe):
                        def body(st):
                            if st.has(0):
                                b = st.t
                                pe.wait_ge(xt_out, b + 1)
                                for k in range(NF):
                                    wait(pe, gelu_done, NF * (b - 1) + k + 1)
                                    pe.matmul(ps_s2[:, k, :], w_fc1[:, k * P:(k + 1) * P], x2_t[:], start=True, stop=True)\
                                        .then_inc(fc1_done, 1)
                            if st.has(-2):
                                b = st.t - 2
                                pe.wait_ge(n3_ready, NT * (b + 1))
                                wait(pe, n3t_out, b)
                                for i in range(NT):
                                    mm = pe.transpose(ps_s1[:, 0, i * P:(i + 1) * P], n3_tok[:, st.buffer(-2), i, :], ident[:])
                                mm.then_inc(n3t_done, 1)
                            if st.has(1):
                                b = st.t + 1
                                pe.wait_ge(xn_ready, NT * (b + 1))
                                wait(pe, xt_out, b)
                                for i in range(NT):
                                    mm = pe.transpose(ps_m[:, i * P:(i + 1) * P], xn[:, st.buffer(1), i, :], ident[:])
                                mm.then_inc(xt_done, 1)
                            if st.has(0):
                                b = st.t
                                pe.wait_ge(gelu_done, NF * (b + 1))
                                wait(pe, summed, b)
                                for i in range(NT):
                                    for k in range(NF):
                                        mm = pe.matmul(ps_pv[:, i * P:(i + 1) * P], hidden[:, k, i * P:(i + 1) * P],
                                                       w_fc2[:, k, :], start=(k == 0), stop=(k == NF - 1))
                                mm.then_inc(fc2_done, 1)
                            if st.has(-2):
                                b = st.t - 2
                                if st.first(-2):
                                    pe.wait_ge(rows_loaded, 16 * 6)
                                pe.wait_ge(n3t_out, b + 1)
                                wait(pe, logits_out, b)
                                for i in range(NT):
                                    mm = pe.matmul(ps_s1[:, 1, i * E:(i + 1) * E], n3_new[:, st.buffer(-2), i * P:(i + 1) * P],
                                                   router_t[:], start=True, stop=True)
                                mm.then_inc(router_done, 1)
                        mlp_steps(pe, body)

                    @block.vector
                    def _(dve):
                        def norm_stats(k, m, src, b):
                            for i in range(NT):
                                dve.bn_stats(stats[:, k, m, i, :], src(i)).then_inc(got[k], 1)
                            wait_apart(dve, got[k], NT * (b + 1), v_zeroed)
                            for i in range(NT):
                                dve.bn_aggr(moments[:, k, m, i, :], stats[:, k, m, i, :]).then_inc(have[k], 1)

                        def gate_row(k, b):
                            return gates[:, bass.ds(b, 1), k * D:(k + 1) * D]

                        def body(st):
                            if st.has(1):
                                b, m = st.t + 1, st.buffer(1)
                                dve.wait_ge(rstd_ready[0], b + 1)
                                wait(dve, xt_done, b - 1)
                                for i in range(NT):
                                    dve.tensor_scalar(xn[:, m, i, :], tile_of(h_sb, b, i), moments[:, 0, m, i, 0:1],
                                                      rstd[:, 0, m, i:i + 1], ALU.subtract, ALU.mult).then_inc(xn_ready, 1)
                            if st.has(-1):
                                b, m = st.t - 1, st.buffer(-1)
                                dve.wait_ge(rstd_ready[1], b + 1)
                                for i in range(NT):
                                    dve.scalar_tensor_tensor(scaled[:, i, :], tile_of(x_sb, b, i), moments[:, 1, m, i, 0:1],
                                                             gate_row(2, b).rearrange("p a d -> p (a d)"),
                                                             ALU.subtract, ALU.mult).then_inc(h3_scaled, 1)
                                wait(dve, n3_ready, NT * (b - 1))
                                dve.wait_ge(h3_scaled, NT * (b + 1))
                                for i in range(NT):
                                    dve.scalar_tensor_tensor(h3[:, m, i, :], scaled[:, i, :], rstd[:, 1, m, i:i + 1],
                                                             gate_row(1, b).rearrange("p a d -> p (a d)"),
                                                             ALU.mult, ALU.add).then_inc(h3_ready, 1)
                            if st.has(2):
                                b2 = st.t + 2
                                wait_apart(dve, xn_ready, NT * b2, v_zeroed)
                                norm_stats(0, st.buffer(2), lambda i: tile_of(h_sb, b2, i), b2)
                            if st.has(-2):
                                b = st.t - 2
                                dve.wait_ge(router_done, b + 1)
                                dve.tensor_copy(logits[:, bass.ds(NT * b, NT), :],
                                                ps_s1[:, 1, 0:NT * E].rearrange("p (i e) -> p i e", e=E))\
                                    .then_inc(logits_out, 1)
                            if st.has(0):
                                b = st.t
                                if st.first(0):
                                    dve.wait_ge(rows_loaded, 16 * 6)
                                x_all = x_sb[:, bass.ds(NT * b, NT), :]
                                dve.wait_ge(fc2_done, b + 1)
                                dve.wait_ge(h_biased, b + 1)
                                dve.tensor_tensor(gated[:], ps_pv[:].rearrange("p (i d) -> p i d", d=D),
                                                  h_sb[:, bass.ds(NT * b, NT), :], ALU.add).then_inc(summed, 1)
                                dve.wait_ge(summed, b + 1)
                                dve.tensor_tensor(gated[:], gated[:], gate_row(0, b).to_broadcast([P, NT, D]), ALU.mult)\
                                    .then_inc(gate_done, 1)
                                dve.wait_ge(gate_done, b + 1)
                                dve.tensor_tensor(x_all, x_all, gated[:], ALU.add).then_inc(x_done, 1)
                                wait_apart(dve, x_done, b + 1, v_zeroed)
                                norm_stats(1, st.buffer(0), lambda i: tile_of(x_sb, b, i), b)
                        mlp_steps(dve, body)

        def route():
            with ExitStack() as own:
                NTOK = B * NT
                shape = [P, NTOK, E]
                capped = sb("capped", shape, until=own)
                score = sb("score", shape, until=own)
                equal = sb("equal", shape, until=own)
                first_of = sb("first_of", [P, E], until=own)
                chosen = sb("chosen", [P, 2] + shape[1:], until=own)
                chosen_any = sb("chosen_any", shape, BF16, until=own)
                best = sb("best", [P, 2, NTOK], until=own)
                tie = sb("tie", [P, NTOK], until=own)
                total = sb("total", [P, NTOK], until=own)
                before_p = sb("before_p", [P, P], BF16, until=own)
                ones_b = sb("ones_b", [P, P], BF16, until=own)
                sums = sb("tile_sums", [P, 2, NTOK // 2 + NTOK, E], until=own)
                slot_of = sb("slot_of", shape, until=own)
                slot_f = sb("slot_f", [P, 2, NTOK], until=own)
                steps_of = sb("steps_of", [P, B * S // SLOTS], until=own)
                over = sb("over", [P, E, B * S // SLOTS], until=own)
                ends = sb("ends", [P, 2, E // 2 + E], until=own)
                base = sb("base", [P, E], until=own)
                tile_no = sb("tile_no", [P, N_TILES], until=own)
                ended = sb("ended", [P, N_TILES, E], until=own)
                n_ended = sb("n_ended", [P, N_TILES], until=own)
                hidden = sb("s_hidden", [P, 2, NF, S], until=own)
                part = sb("part", [P, NT, D], until=own)

                gate_loaded, tables, tables2, capped_ready = sem("gate_loaded"), sem("tables"), sem("tables2"), sem("capped_ready")
                exped, routing, chosen_ready, counted = sem("exped"), sem("routing"), sem("chosen_ready"), sem("counted")
                slots_ready, scattered, renumbered = sem("slots_ready"), sem("scattered"), sem("renumbered")
                l1_done, relu_done, l2_done = sem("s_l1_done"), sem("s_relu_done"), sem("s_l2_done")
                bank_free, part_steps = sem("s_bank_free"), sem("part_steps")

                def s_steps(eng, body):
                    pipeline(eng, body, 0, B, 2, B)

                with nc.Block() as block:
                    @block.sync
                    def _(sp):
                        sp.dma_start(gate_b[:], mod_d[:, 5 * D:6 * D].partition_broadcast(P)).then_inc(gate_loaded, 16)
                        sp.wait_ge(gate_loaded, 16)

                    @block.gpsimd
                    def _(pool):
                        def iota(dst, **pattern):
                            return pool.iota(dst, allow_small_or_imprecise_dtypes=True, **pattern).then_inc(tables, 1)
                        pool.memset(before_p[:], 1.0).then_inc(tables2, 1)
                        pool.memset(ones_b[:], 1.0).then_inc(tables, 1)
                        pool.memset(sums[:], 0.0).then_inc(tables, 1)
                        pool.memset(ends[:], 0.0).then_inc(tables, 1)
                        pool.wait_ge(tables2, 1)
                        pool.affine_select(out=before_p[:], in_=before_p[:], compare_op=ALU.is_ge, fill=0.0, base=-1,
                                           pattern=[[1, P]], channel_multiplier=-1).then_inc(tables, 1)
                        iota(first_of[:], pattern=[[-1, E]], base=E, channel_multiplier=0)
                        iota(steps_of[:], pattern=[[SLOTS, B * S // SLOTS]], base=0, channel_multiplier=0)
                        iota(tile_no[:], pattern=[[1, N_TILES]], base=0, channel_multiplier=0)
                        for c in range(2):
                            if c == 0:
                                pool.wait_ge(slots_ready, 1)
                            else:
                                pool.wait_ge(scattered, 16 * NTOK)
                                pool.iota(n3x[:, :, D:D + 1].bitcast(I32), pattern=[[P, NTOK], [0, 1]], base=B * S,
                                          channel_multiplier=1).then_inc(renumbered, 1)
                                pool.wait_ge(renumbered, 1)
                            for n in range(NTOK):
                                pool.indirect_dma_start(slots_d[:], bass.IndirectOffsetOnAxis(ap=slots[:, c, n:n + 1], axis=0),
                                                        n3x[:, n, :], None).then_inc(scattered, 16)
                        pool.wait_ge(scattered, 2 * 16 * NTOK)

                    @block.scalar
                    def _(act):
                        act.wait_ge(capped_ready, 1)
                        act.activation(score[:], capped[:], ACT.Exp, scale=-1.0).then_inc(exped, 1)

                        def body(st):
                            if st.has(0):
                                b = st.t
                                for k in range(NF):
                                    act.wait_ge(l1_done, NF * b + k + 1)
                                    if k == 0:
                                        wait(act, l2_done, b - 1)
                                    act.activation(hidden[:, st.buffer(0), k, :], ps_s2[:, k, :], ACT.Relu,
                                                   bias=col("sb1", k)).then_inc(relu_done, 1)
                        s_steps(act, body)

                    @block.tensor
                    def _(pe):
                        def body(st):
                            if st.first(-1):
                                pe.wait_ge(chosen_ready, 1)
                                pe.wait_ge(tables, 7)
                                both = chosen_any[:].rearrange("p n e -> p (n e)")
                                pe.matmul(ps_m[:, 0:NTOK * E], before_p[:], both, start=True, stop=True)
                                pe.matmul(ps_m[:, NTOK * E:2 * NTOK * E], ones_b[:], both, start=True, stop=True)\
                                    .then_inc(counted, 1)
                            if st.has(0):
                                b = st.t
                                for k in range(NF):
                                    wait(pe, relu_done, NF * (b - 1) + k + 1)
                                    pe.matmul(ps_s2[:, k, :], shared_w1[:, k * P:(k + 1) * P], n3_t[:, bass.ds(S * b, S)],
                                              start=True, stop=True).then_inc(l1_done, 1)
                            if st.has(-1):
                                b = st.t - 1
                                pe.wait_ge(relu_done, NF * (b + 1))
                                wait(pe, bank_free, b)
                                for i in range(NT):
                                    for k in range(NF):
                                        mm = pe.matmul(ps_pv[:, i * P:(i + 1) * P],
                                                       hidden[:, st.buffer(-1), k, i * P:(i + 1) * P],
                                                       shared_w2[:, k, :], start=(k == 0), stop=(k == NF - 1))
                                mm.then_inc(l2_done, 1)
                        s_steps(pe, body)

                    @block.vector
                    def _(dve):
                        done = iter(range(1, 100))

                        def chain(op):
                            op.then_inc(routing, 1)
                            dve.wait_ge(routing, next(done))

                        def over_experts(v):
                            return v.unsqueeze(2).to_broadcast(shape)

                        dve.tensor_scalar(capped[:], logits[:], -80.0, None, ALU.max).then_inc(capped_ready, 1)
                        dve.wait_ge(exped, 1)
                        chain(dve.tensor_scalar(capped[:], score[:], 1.0, None, ALU.add))
                        chain(dve.reciprocal(score[:], capped[:]))
                        dve.wait_ge(tables, 7)
                        src = score
                        for c in range(2):
                            chain(dve.tensor_reduce(best[:, c], src[:], AXIS.X, ALU.max))
                            chain(dve.tensor_tensor(equal[:], src[:], over_experts(best[:, c]), ALU.is_equal))
                            chain(dve.tensor_tensor(equal[:], equal[:], first_of[:].unsqueeze(1).to_broadcast(shape), ALU.mult))
                            chain(dve.tensor_reduce(tie[:], equal[:], AXIS.X, ALU.max))
                            chain(dve.tensor_tensor(chosen[:, c], equal[:], over_experts(tie[:]), ALU.is_equal))
                            if c == 0:
                                chain(dve.scalar_tensor_tensor(capped[:], chosen[:, 0], -4.0, score[:], ALU.mult, ALU.add))
                                src = capped
                        dve.tensor_tensor(chosen_any[:], chosen[:, 0], chosen[:, 1], ALU.add).then_inc(chosen_ready, 1)
                        dve.wait_ge(counted, 1)
                        pad = NTOK // 2
                        prefix = ps_m[:, 0:NTOK * E].rearrange("p (n e) -> p n e", e=E)
                        tile_total = ps_m[:, NTOK * E:2 * NTOK * E].rearrange("p (n e) -> p n e", e=E)
                        chain(dve.tensor_copy(sums[:, 0, pad:], tile_total))
                        at, shift = 0, 1
                        while shift < NTOK:
                            chain(dve.tensor_tensor(sums[:, 1 - at, pad:], sums[:, at, pad:],
                                                    sums[:, at, pad - shift:pad - shift + NTOK], ALU.add))
                            at, shift = 1 - at, 2 * shift
                        counts = sums[:, at, pad + NTOK - 1]
                        chain(dve.tensor_tensor(over[:], counts.unsqueeze(2).to_broadcast([P, E, B * S // SLOTS]),
                                                steps_of[:].unsqueeze(1).to_broadcast([P, E, B * S // SLOTS]), ALU.is_gt))
                        chain(dve.tensor_reduce(ends[:, 0, E // 2:], over[:], AXIS.X, ALU.add))
                        chain(dve.tensor_scalar(base[:], ends[:, 0, E // 2:], -1.0, None, ALU.mult))
                        at2, shift = 0, 1
                        while shift < E:
                            chain(dve.tensor_tensor(ends[:, 1 - at2, E // 2:], ends[:, at2, E // 2:],
                                                    ends[:, at2, E // 2 - shift:E // 2 - shift + E], ALU.add))
                            at2, shift = 1 - at2, 2 * shift
                        end = ends[:, at2, E // 2:]
                        chain(dve.tensor_tensor(base[:], base[:], end, ALU.add))
                        chain(dve.tensor_scalar(base[:], base[:], float(SLOTS), None, ALU.mult))
                        chain(dve.tensor_tensor(slot_of[:], sums[:, at, pad:], tile_total, ALU.subtract))
                        chain(dve.tensor_tensor(slot_of[:], slot_of[:], prefix, ALU.add))
                        chain(dve.tensor_tensor(slot_of[:], slot_of[:], base[:].unsqueeze(1).to_broadcast(shape), ALU.add))
                        for c in range(2):
                            chain(dve.tensor_tensor(equal[:], chosen[:, c], slot_of[:], ALU.mult))
                            chain(dve.tensor_reduce(slot_f[:, c], equal[:], AXIS.X, ALU.add))
                        dve.tensor_copy(slots[:], slot_f[:]).then_inc(slots_ready, 1)
                        chain(dve.tensor_tensor(total[:], best[:, 0], best[:, 1], ALU.add))
                        chain(dve.tensor_scalar(total[:], total[:], 1e-6, None, ALU.add))
                        chain(dve.reciprocal(tie[:], total[:]))
                        for c in range(2):
                            chain(dve.tensor_tensor(picked_w[:, c], best[:, c], tie[:], ALU.mult))
                        of_tile = [P, N_TILES, E]
                        chain(dve.tensor_tensor(ended[:], tile_no[:].unsqueeze(2).to_broadcast(of_tile),
                                                end.unsqueeze(1).to_broadcast(of_tile), ALU.is_ge))
                        chain(dve.tensor_reduce(n_ended[:], ended[:], AXIS.X, ALU.add))
                        chain(dve.tensor_scalar(n_ended[:], n_ended[:], float(E - 1), None, ALU.min))
                        chain(dve.tensor_copy(tile_expert[:], n_ended[:]))

                        dve.wait_ge(gate_loaded, 16)

                        def body(st):
                            if st.has(-1):
                                b = st.t - 1
                                dve.wait_ge(l2_done, b + 1)
                                wait(dve, part_steps, 2 * b)
                                dve.tensor_tensor(part[:], ps_pv[:].rearrange("p (i d) -> p i d", d=D),
                                                  sb2_all[:].unsqueeze(1).to_broadcast([P, NT, D]), ALU.add).then_inc(bank_free, 1)
                                dve.wait_ge(bank_free, b + 1)
                                dve.tensor_tensor(part[:], part[:], gate_b[:, bass.ds(b, 1), :].to_broadcast([P, NT, D]), ALU.mult)\
                                    .then_inc(part_steps, 1)
                                dve.wait_ge(part_steps, 2 * b + 1)
                                dve.tensor_tensor(h_sb[:, bass.ds(NT * b, NT), :], x_sb[:, bass.ds(NT * b, NT), :], part[:], ALU.add)\
                                    .then_inc(part_steps, 1)
                        s_steps(dve, body)

        def experts():
            HALVES, BUF = SLOTS // P, 4
            with ExitStack() as own:
                w = sb("w_tile", [P, BUF, EW], until=own)
                bias2 = sb("bias2", [P, BUF, D], until=own)
                rows = sb("rows", [P, BUF, HALVES, ROW], until=own)
                tok_t = sb("tok_t", [P, BUF, SLOTS], until=own)
                hidden = sb("x_hidden", [P, BUF, NF, SLOTS], until=own)
                res = sb("res", [P, BUF, HALVES, D], until=own)
                target = sb("target", [P, BUF, HALVES], U32, until=own)
                rows_in = [sem(f"rows_in{k}") for k in range(BUF)]
                w_in = [sem(f"w_in{k}") for k in range(BUF)]
                put = [sem(f"put{k}") for k in range(BUF)]
                turned, tok_out, l1_done, relu_done = sem("turned"), sem("tok_out"), sem("x_l1_done"), sem("x_relu_done")
                l2_done, res_ready = sem("x_l2_done"), sem("res_ready")
                slots_r = slots_d.rearrange("(t c p) w -> p t c w", p=P, c=HALVES)

                def loads(t, k):
                    return 16 // BUF * (t - k) + 16

                def x_steps(eng, body):
                    pipeline(eng, body, -1, N_TILES, BUF, (N_TILES - 1) // BUF * BUF, unroll=BUF, count=N_TILES)

                def tiles(eng, body):
                    pipeline(eng, body, 0, N_TILES - 1, BUF, N_TILES // BUF * BUF, unroll=BUF, count=N_TILES)

                def tok_bank(k):
                    return (ps_m, ps_pv)[k % 2]

                with nc.Block() as block:
                    @block.sync
                    def _(sp):
                        def body(st):
                            t, k = st.t, st.buffer(0, BUF)
                            wait_apart(sp, res_ready, t - BUF + 1, v_zeroed)
                            sp.dma_start(rows[:, k], slots_r[:, bass.ds(t, 1), :, :].rearrange("p a c w -> p (a c) w"))\
                                .then_inc(rows_in[k], 16)
                            e = sp.value_load(tile_expert[0:1, bass.ds(t, 1)], min_val=0, max_val=E - 1)
                            sp.dma_start(w[:, k], a["ew"][bass.ds(e, 1), :, :].rearrange("a p w -> p (a w)")).then_inc(w_in[k], 16)
                            sp.dma_start(bias2[:, k], a["eb2"][bass.ds(e, 1), :].rearrange("a d -> (a d)").partition_broadcast(P))\
                                .then_inc(w_in[k], 16)
                        tiles(sp, body)

                    @block.gpsimd
                    def _(pool):
                        def body(st):
                            t, k = st.t, st.buffer(0, BUF)
                            wait_apart(pool, res_ready, t + 1, v_zeroed)
                            for c in range(HALVES):
                                pool.indirect_dma_start(y_d[:], bass.IndirectOffsetOnAxis(
                                    ap=target[:, k, c:c + 1], axis=0), res[:, k, c, :], None).then_inc(put[k], 16)
                        tiles(pool, body)
                        for k in range(BUF):
                            pool.wait_ge(put[k], 16 * HALVES * len(range(k, N_TILES, BUF)))

                    @block.scalar
                    def _(act):
                        def body(st):
                            if st.has(1):
                                t, k = st.t + 1, st.buffer(1, BUF)
                                act.wait_ge(turned, t + 1)
                                wait(act, l1_done, NF // 2 * (t - BUF + 1))
                                act.activation(tok_t[:, k], tok_bank(k)[:, 0:SLOTS], ACT.Copy, scale=col("norm_w"))\
                                    .then_inc(tok_out, 1)
                            if st.has(0):
                                t, k = st.t, st.buffer(0, BUF)
                                for f in range(NF):
                                    if f % 2 == 0:
                                        act.wait_ge(l1_done, NF // 2 * t + f // 2 + 1)
                                    if f == 0:
                                        wait(act, l2_done, t - BUF + 1)
                                    act.activation(hidden[:, k, f], ps_s2[:, 2 * (k % 2) + f // 2, (f % 2) * SLOTS:(f % 2 + 1) * SLOTS],
                                                   ACT.Relu, bias=w[:, k, FF + NF * D + f:FF + NF * D + f + 1]).then_inc(relu_done, 1)
                        x_steps(act, body)

                    @block.tensor
                    def _(pe):
                        def body(st):
                            if st.has(1):
                                t, k = st.t + 1, st.buffer(1, BUF)
                                pe.wait_ge(rows_in[k], loads(t, k))
                                wait(pe, tok_out, t - 1)
                                for c in range(HALVES):
                                    mm = pe.transpose(tok_bank(k)[:, c * P:(c + 1) * P], rows[:, k, c, 0:D], ident[:])
                                mm.then_inc(turned, 1)
                            if st.has(0):
                                t, k = st.t, st.buffer(0, BUF)
                                pe.wait_ge(w_in[k], 2 * loads(t, k))
                                pe.wait_ge(tok_out, t + 1)
                                wait(pe, relu_done, NF * (t - 1))
                                for f in range(NF):
                                    mm = pe.matmul(ps_s2[:, 2 * (k % 2) + f // 2, (f % 2) * SLOTS:(f % 2 + 1) * SLOTS],
                                              w[:, k, f * P:(f + 1) * P], tok_t[:, k], start=True, stop=True)
                                    if f % 2 == 1:
                                        mm.then_inc(l1_done, 1)
                            if st.has(-1):
                                t, k = st.t - 1, st.buffer(-1, BUF)
                                pe.wait_ge(relu_done, NF * (t + 1))
                                wait(pe, res_ready, t - 1)
                                for c in range(HALVES):
                                    for f in range(NF):
                                        mm = pe.matmul(ps_s1[:, k % 2, c * P:(c + 1) * P], hidden[:, k, f, c * P:(c + 1) * P],
                                                       w[:, k, FF + f * D:FF + (f + 1) * D], start=(f == 0), stop=(f == NF - 1))
                                mm.then_inc(l2_done, 1)
                        x_steps(pe, body)

                    @block.vector
                    def _(dve):
                        def body(st):
                            t, k = st.t, st.buffer(0, BUF)
                            wait(dve, put[k], 2 * (loads(t, k) - 16))
                            dve.wait_ge(rows_in[k], loads(t, k))
                            dve.tensor_copy(target[:, k], rows[:, k, :, D:D + 1].rearrange("p c a -> p (c a)").bitcast(U32))
                            dve.wait_ge(l2_done, t + 1)
                            dve.tensor_tensor(res[:, k], ps_s1[:, k % 2, 0:HALVES * D].rearrange("p (c d) -> p c d", d=D),
                                              bias2[:, k].unsqueeze(1).to_broadcast([P, HALVES, D]), ALU.add).then_inc(res_ready, 1)
                        tiles(dve, body)

        def combine():
            with ExitStack() as own:
                got = sb("got", [P, 2, 2, NT, D], until=own)
                weighted = sb("weighted", [P, 2, 2, NT, D], until=own)
                result_b = sb("result_b", [P, 2, NT, D], until=own)
                loaded = [[sem(f"got{c}{k}") for k in range(2)] for c in range(2)]
                mixed, by_first, by_second, final = sem("mixed"), sem("by_first"), sem("by_second"), sem("final")
                stored = [sem("stored0"), sem("stored1")]
                y_r = y_d[0:2 * B * S, :].rearrange("(c n p) d -> p c n d", p=P, c=2)
                wide = [P, NT, D]

                def c_steps(eng, body):
                    pipeline(eng, body, 0, B - 1, 2, B)

                def weight_of(c, b):
                    return picked_w[:, c, bass.ds(NT * b, NT)].unsqueeze(2).to_broadcast(wide)

                with nc.Block() as block:
                    @block.sync
                    def _(sp):
                        def body(st):
                            b, k = st.t, st.buffer(0)
                            wait(sp, by_first, NT * (b - 1))
                            sp.dma_start(got[:, 0, k], y_r[:, 0, bass.ds(NT * b, NT), :]).then_inc(loaded[0][k], 16)
                            wait(sp, by_second, b - 1)
                            sp.dma_start(got[:, 1, k], y_r[:, 1, bass.ds(NT * b, NT), :]).then_inc(loaded[1][k], 16)
                        c_steps(sp, body)

                    @block.scalar
                    def _(act):
                        def body(st):
                            if st.has(0):
                                b, k = st.t, st.buffer(0)
                                wait(act, final, b - 1)
                                wait_apart(act, loaded[0][k], 8 * (b - k) + 16, v_zeroed)
                                for i in range(NT):
                                    act.activation(weighted[:, 0, k, i], got[:, 0, k, i], ACT.Copy,
                                                   scale=picked_w[:, 0, bass.ds(NT * b + i, 1)]).then_inc(by_first, 1)
                            if st.has(-1):
                                b, k = st.t - 1, st.buffer(-1)
                                wait_apart(act, final, b + 1, v_zeroed)
                                act.dma_start(out_tok[:, bass.ds(NT * b, NT), :], result_b[:, k]).then_inc(stored[k], 16)
                        pipeline(act, body, 0, B, 2, B)
                        for half_stored in stored:
                            act.wait_ge(half_stored, 16 * B // 2)

                    @block.gpsimd
                    def _(pool):
                        def body(st):
                            b, k = st.t, st.buffer(0)
                            pool.wait_ge(loaded[1][k], 8 * (b - k) + 16)
                            wait(pool, mixed, 2 * b - 3)
                            pool.tensor_tensor(weighted[:, 1, k], got[:, 1, k], weight_of(1, b), ALU.mult).then_inc(by_second, 1)
                        c_steps(pool, body)

                    @block.vector
                    def _(dve):
                        def body(st):
                            b, k = st.t, st.buffer(0)
                            wait(dve, final, b - 1)
                            dve.wait_ge(by_first, NT * (b + 1))
                            dve.wait_ge(by_second, b + 1)
                            dve.tensor_tensor(weighted[:, 0, k], weighted[:, 0, k], weighted[:, 1, k], ALU.add).then_inc(mixed, 1)
                            dve.wait_ge(mixed, 2 * b + 1)
                            dve.tensor_tensor(weighted[:, 0, k], weighted[:, 0, k], gate_b[:, bass.ds(b, 1), :].to_broadcast(wide), ALU.mult)\
                                .then_inc(mixed, 1)
                            dve.wait_ge(mixed, 2 * b + 2)
                            wait(dve, stored[k], 8 * (b - k))
                            dve.tensor_tensor(result_b[:, k], weighted[:, 0, k], h_sb[:, bass.ds(NT * b, NT), :], ALU.add)\
                                .then_inc(final, 1)
                        c_steps(dve, body)

        setup()
        attend()
        front.close()
        router_t = sb("router_t", [P, E])
        logits = sb("logits", [P, B * NT, E])
        n3x = sb("n3x", [P, B * NT, ROW])
        n3_t = sb("n3_t", [P, B * S])
        shared_w1 = sb("shared_w1", [P, FF])
        shared_w2 = sb("shared_w2", [P, NF, D])
        gate_b = sb("gate_b", [P, B, D])
        sb2_all = sb("sb2_all", [P, D])
        slots_d = dram("slots_d", (N_SLOTS, ROW))
        y_d = dram("y_d", (2 * B * S + N_SLOTS, D))
        mlp()
        route()
        experts()
        combine()


def kernel(**inputs):
    import numpy as np
    import concourse.bacc as bacc
    from concourse.bass_utils import run_bass_kernel_spmd

    g = {k[3:]: np.asarray(v) for k, v in inputs.items()}
    at = {k[5:]: v for k, v in g.items() if k.startswith("attn_")}
    ff = {k[4:]: v for k, v in g.items() if k.startswith("ffn_")}

    def heads_last(v):
        return v.T.reshape(-1, 1)

    def over_partitions(v, k):
        return v.reshape(k, P).T

    arrays = {
        "x": at["hidden_states"],
        "c_t": g["c"].T,
        "w_mod": g["wmod"],
        "u_t": np.stack([at[n + "_U"].reshape(D, PAIRS, 2 * RANK).transpose(2, 1, 0) for n in "qkv"], axis=1),
        "v_pairs": np.stack([at[n + "_V"].reshape(PAIRS, 2, RANK, DH).transpose(1, 2, 0, 3) for n in "qkv"], axis=2),
        "out_ut": at["out_U"].T,
        "out_v": at["out_V"],
        "fc1_ut": at["fc1_U"].T,
        "fc1_v": at["fc1_V"],
        "fc2_ut": at["fc2_U"].T,
        "fc2_v": at["fc2_V"],
        "out_b": at["out_b"],
        "fc2_b": at["fc2_b"],
        "sb2": ff["sb2"],
        "cols": np.concatenate([
            at["ln1_g"].reshape(P, 1), at["ln1_b"].reshape(P, 1), heads_last(at["q_b"]), heads_last(at["k_b"]),
            at["v_b"].reshape(P, 1), at["ln2_g"].reshape(P, 1), at["ln2_b"].reshape(P, 1),
            ff["norm_weight"].reshape(P, 1), over_partitions(at["fc1_b"], NF), over_partitions(ff["sb1"], NF),
            over_partitions(ff["eb1"], E * NF)], axis=1),
        "router_t": ff["router_w"].T,
        "sw1": ff["sw1"],
        "sw2": ff["sw2"].reshape(NF, P, D).transpose(1, 0, 2),
        "ew": np.concatenate([ff["ew1"], ff["ew2"].reshape(E, NF, P, D).transpose(0, 2, 1, 3).reshape(E, P, NF * D),
                              ff["eb1"].reshape(E, NF, P).transpose(0, 2, 1)], axis=2),
        "eb2": ff["eb2"],
    }
    nc = bacc.Bacc("TRN2", target_bir_lowering=False, num_devices=1)
    feed, aps = {}, {}
    for name, v in arrays.items():
        v = np.ascontiguousarray(v)
        feed["in_" + name] = v
        aps[name] = nc.dram_tensor("in_" + name, v.shape, mybir.dt.from_np(v.dtype), kind="ExternalInput").ap()
    result = nc.dram_tensor("result", (B, S, D), F32, kind="ExternalOutput").ap()
    adaln_block(nc, aps, result)
    r = run_bass_kernel_spmd(nc, [feed], core_ids=[0])
    return r.results[0]["result"]
```
